# Optimizing a Trainium2 kernel written in Bass

```python
import numpy as np
import jax
import jax.numpy as jnp

def _softmax(x, axis=-1):
    return jax.nn.softmax(x, axis=axis)

def _gelu(x):
    return jax.nn.gelu(x, approximate=True)

def _silu(x):
    return jax.nn.silu(x)

def _sigmoid(x):
    return jax.nn.sigmoid(x)

def _layernorm(x, axis=-1, eps=1e-05):
    m = jnp.mean(x, axis=axis, keepdims=True)
    v = jnp.var(x, axis=axis, keepdims=True)
    return (x - m) / jnp.sqrt(v + eps)

def _scatter_add(tgt, idx, src, axis=0):
    return tgt.at[idx].add(src)

def _segment_sum(src, seg, n):
    return jax.ops.segment_sum(src, seg, n)
kernel_name = 'mk_vit_tower_postln_d1_tok_img768_r4_ac5911'

def setup_inputs(seed: int=0):
    np.random.seed(seed)
    _w = jnp.asarray

    def _rec_inputs():
        import jax
        import jax.numpy as jnp
        _rk = jax.random.key(seed)
        x = -0.00040386 + 0.999972 * jax.random.normal(jax.random.fold_in(_rk, 1), (32, 64, 64, 3), jnp.float32)
        return x
    x = _rec_inputs()

    def _L0_tok_setup():
        import jax, jax.numpy as jnp
        import numpy as np
        IMG = 64
        PATCH = 16
        C = 3
        D = 192
        NP_ = (IMG // PATCH) ** 2
        B = 64

        def _patchify(x):
            Bn, H, Wd, Cn = x.shape
            hp, wp = (H // PATCH, Wd // PATCH)
            x = x.reshape(Bn, hp, PATCH, wp, PATCH, Cn)
            x = x.transpose(0, 1, 3, 2, 4, 5)
            return x.reshape(Bn, hp * wp, PATCH * PATCH * Cn)
        key = jax.random.key(seed)
        k1, k2, k3 = jax.random.split(key, 3)
        x = jax.random.normal(k1, (B, IMG, IMG, C), dtype=jnp.float32)
        patch_dim = C * PATCH * PATCH
        W = jax.random.normal(k2, (patch_dim, D), dtype=jnp.float32) / np.sqrt(patch_dim)
        b = jnp.zeros((D,), dtype=jnp.float32)
        pos_emb = jax.random.normal(k3, (NP_, D), dtype=jnp.float32) * 0.02
        return {'x': x, 'W': W, 'b': b, 'pos_emb': pos_emb}
    _L0_tok_all = _L0_tok_setup()
    _L0_tok_in = {k: v for k, v in _L0_tok_all.items() if k in ('W', 'b', 'pos_emb')}
    del _L0_tok_all

    def _L0_attn_setup():
        import jax, jax.numpy as jnp
        import numpy as np
        SEQ, BATCH, EMBED = (512, 4, 192)
        NUM_HEADS = 12
        HEAD_DIM = EMBED // NUM_HEADS
        SCALING = HEAD_DIM ** (-0.5)
        key = jax.random.key(seed)
        ks = jax.random.split(key, 9)
        std = 0.02
        d = {'x': jax.random.normal(ks[0], (SEQ, BATCH, EMBED), dtype=jnp.float32)}
        for i, n in enumerate(['q', 'k', 'v', 'out']):
            d[f'W{n}'] = jax.random.normal(ks[1 + 2 * i], (EMBED, EMBED), dtype=jnp.float32) * std
            d[f'b{n}'] = jax.random.normal(ks[2 + 2 * i], (EMBED,), dtype=jnp.float32) * std
        return d
    _L0_attn_all = _L0_attn_setup()
    _L0_attn_in = {k: v for k, v in _L0_attn_all.items() if k in ('Wq', 'bq', 'Wk', 'bk', 'Wv', 'bv', 'Wout', 'bout')}
    del _L0_attn_all

    def _L0_ffn_setup():
        import jax, jax.numpy as jnp
        import numpy as np
        E = 8
        K = 2
        D = 192
        I = 768
        B, S = (2, 512)
        key = jax.random.key(seed)
        ks = jax.random.split(key, 8)
        x = jax.random.normal(ks[0], (B, S, D), dtype=jnp.float32)
        W1 = jax.random.normal(ks[1], (E, D, I), dtype=jnp.float32) * 0.02
        b1 = jnp.zeros((E, I), dtype=jnp.float32)
        W2 = jax.random.normal(ks[2], (E, I, D), dtype=jnp.float32) * 0.02
        b2 = jnp.zeros((E, D), dtype=jnp.float32)
        Wr = jax.random.normal(ks[3], (D, E), dtype=jnp.float32) * 0.02
        br = jnp.zeros((E,), dtype=jnp.float32)
        return {'x': x, 'W1': W1, 'b1': b1, 'W2': W2, 'b2': b2, 'Wr': Wr, 'br': br}
    _L0_ffn_all = _L0_ffn_setup()
    _L0_ffn_in = {k: v for k, v in _L0_ffn_all.items() if k in ('W1', 'b1', 'W2', 'b2', 'Wr', 'br')}
    del _L0_ffn_all
    return {'x': x, 'L0_tok_W': _L0_tok_in['W'], 'L0_tok_b': _L0_tok_in['b'], 'L0_tok_pos_emb': _L0_tok_in['pos_emb'], 'L0_attn_Wq': _L0_attn_in['Wq'], 'L0_attn_bq': _L0_attn_in['bq'], 'L0_attn_Wk': _L0_attn_in['Wk'], 'L0_attn_bk': _L0_attn_in['bk'], 'L0_attn_Wv': _L0_attn_in['Wv'], 'L0_attn_bv': _L0_attn_in['bv'], 'L0_attn_Wout': _L0_attn_in['Wout'], 'L0_attn_bout': _L0_attn_in['bout'], 'L0_ffn_W1': _L0_ffn_in['W1'], 'L0_ffn_b1': _L0_ffn_in['b1'], 'L0_ffn_W2': _L0_ffn_in['W2'], 'L0_ffn_b2': _L0_ffn_in['b2'], 'L0_ffn_Wr': _L0_ffn_in['Wr'], 'L0_ffn_br': _L0_ffn_in['br']}

def reference(x, L0_tok_W, L0_tok_b, L0_tok_pos_emb, L0_attn_Wq, L0_attn_bq, L0_attn_Wk, L0_attn_bk, L0_attn_Wv, L0_attn_bv, L0_attn_Wout, L0_attn_bout, L0_ffn_W1, L0_ffn_b1, L0_ffn_W2, L0_ffn_b2, L0_ffn_Wr, L0_ffn_br):
    import jax
    import jax.numpy as jnp

    def _L0_tok_ref(x, W, b, pos_emb):
        import jax, jax.numpy as jnp
        import numpy as np
        IMG = 64
        PATCH = 16
        C = 3
        D = 192
        NP_ = (IMG // PATCH) ** 2
        B = 64

        def _patchify(x):
            Bn, H, Wd, Cn = x.shape
            hp, wp = (H // PATCH, Wd // PATCH)
            x = x.reshape(Bn, hp, PATCH, wp, PATCH, Cn)
            x = x.transpose(0, 1, 3, 2, 4, 5)
            return x.reshape(Bn, hp * wp, PATCH * PATCH * Cn)
        patches = _patchify(x)
        proj = jnp.einsum('bnd,de->bne', patches, W) + b
        return proj + pos_emb[None, :, :]

    def _L0_attn_ref(x, Wq, bq, Wk, bk, Wv, bv, Wout, bout):
        import jax, jax.numpy as jnp
        import numpy as np
        SEQ, BATCH, EMBED = (512, 4, 192)
        NUM_HEADS = 12
        HEAD_DIM = EMBED // NUM_HEADS
        SCALING = HEAD_DIM ** (-0.5)
        T, B, E = x.shape
        H, Dh = (NUM_HEADS, HEAD_DIM)
        q = (x @ Wq.T + bq) * SCALING
        k = x @ Wk.T + bk
        v = x @ Wv.T + bv
        q = q.reshape(T, B * H, Dh).transpose(1, 0, 2)
        k = k.reshape(T, B * H, Dh).transpose(1, 0, 2)
        v = v.reshape(T, B * H, Dh).transpose(1, 0, 2)
        scores = jnp.einsum('bqd,bkd->bqk', q, k)
        probs = jax.nn.softmax(scores.astype(jnp.float32), axis=-1).astype(scores.dtype)
        attn = jnp.einsum('bqk,bkd->bqd', probs, v)
        attn = attn.transpose(1, 0, 2).reshape(T, B, E)
        return attn @ Wout.T + bout

    def _L0_ffn_ref(x, W1, b1, W2, b2, Wr, br):
        import jax, jax.numpy as jnp
        import numpy as np
        E = 8
        K = 2
        D = 192
        I = 768
        B, S = (2, 512)
        Bv, Sv, Dv = x.shape
        xf = x.reshape(-1, Dv)
        logits = xf @ Wr + br
        gates = jax.nn.softmax(logits, axis=-1)
        top_g, top_i = jax.lax.top_k(gates, K)
        out = jnp.zeros_like(xf)
        for e in range(E):
            w_e = jnp.sum(top_g * (top_i == e), axis=-1)
            h = jax.nn.gelu(xf @ W1[e] + b1[e], approximate=False)
            y = h @ W2[e] + b2[e]
            out = out + w_e[:, None] * y
        return out.reshape(Bv, Sv, Dv)
    h = _L0_tok_ref(x, L0_tok_W, L0_tok_b, L0_tok_pos_emb)
    h = _layernorm(h + _L0_attn_ref(h, L0_attn_Wq, L0_attn_bq, L0_attn_Wk, L0_attn_bk, L0_attn_Wv, L0_attn_bv, L0_attn_Wout, L0_attn_bout), axis=-1)
    h = _layernorm(h + _L0_ffn_ref(h, L0_ffn_W1, L0_ffn_b1, L0_ffn_W2, L0_ffn_b2, L0_ffn_Wr, L0_ffn_br), axis=-1)
    return h

_drawn_inputs = setup_inputs


def setup_inputs(seed=0):
    import zlib

    import numpy as np

    out = dict(_drawn_inputs(seed))
    spreads = {'L0_tok_b': (0.0, 0.1),
     'L0_ffn_b1': (0.0, 0.8),
     'L0_ffn_b2': (0.0, 0.309),
     'L0_ffn_br': (0.0, 0.331)}
    factors = {'L0_tok_pos_emb': 2.764,
     'L0_attn_Wq': 8.0,
     'L0_attn_bq': 8.0,
     'L0_attn_Wk': 8.0,
     'L0_attn_bk': 8.0,
     'L0_attn_Wv': 3.346,
     'L0_attn_bv': 8.0,
     'L0_attn_Wout': 3.262,
     'L0_ffn_W1': 2.774}
    for name, (base, spread) in spreads.items():
        noise = np.random.default_rng([zlib.crc32(name.encode()), seed]).standard_normal(out[name].shape)
        drawn = base * np.exp(spread * noise) if base else spread * noise
        out[name] = jnp.asarray(drawn.astype(out[name].dtype))
    for name, factor in factors.items():
        out[name] = (out[name] * factor).astype(out[name].dtype)
    return out
```

```python
from contextlib import ExitStack

import concourse.bass as bass
from concourse import mybir

F32 = mybir.dt.float32
F32R = mybir.dt.float32r
U32 = mybir.dt.uint32
ALU = mybir.AluOpType
ACT = mybir.ActivationFunctionType
AX = mybir.AxisListType.X

P = 128
PATCH = 16
CHANNELS = 3
HEADS = 12
TOP_K = 2
LN_EPS = 1e-5
BANK = 512


def build(nc, x, tok_w, tok_b, pos, wq, bq, wk, bk, wv, bv, wout, bout, w1, b1, w2, b2, wr, br, out):
    IMGS, SIDE = x.shape[0], x.shape[1]
    E = tok_w.shape[1]
    NP = SIDE // PATCH
    PATCHES = NP * NP
    TOKENS = IMGS * PATCHES
    PATCH_DIM = PATCH * PATCH * CHANNELS
    RUN = PATCH * CHANNELS
    KC = PATCH_DIM // P
    HD = E // HEADS
    EH = E // 2
    HG = 4
    GE = HG * HD
    GROUPS = HEADS // HG
    EA, EB = P, E - P
    EXPERTS, HID = w1.shape[0], w1.shape[2]
    HT = HID // P
    HALF = TOKENS // 2
    SCALE = float(HD) ** -0.5
    assert NP * IMGS == P and KC * P == PATCH_DIM and 2 * EB == P and GE == EB and GROUPS == 3
    assert EXPERTS == 8 and TOKENS == BANK and NP == 4 and HT == 6

    W1A, W1B = slice(0, HID), slice(HID, 2 * HID)

    with ExitStack() as ctx:
        def sb(name, shape, dt=F32):
            return ctx.enter_context(nc.sbuf_tensor(name, shape, dt))

        def sem(name):
            return ctx.enter_context(nc.semaphore(name))

        bank = [ctx.enter_context(nc.psum_tensor(f"bank{i}", [P, BANK], F32)) for i in range(8)]

        ident = sb("ident", [P, P])
        repeat = sb("repeat", [P, HG, IMGS])
        pos_sb = sb("pos_sb", [PATCHES + 1, E])
        pos_sel = sb("pos_sel", [PATCHES + 1, NP, NP, IMGS])
        w_nat = [sb(f"{n}_nat", [EH, 2, E]) for n in ("wq", "wk", "wv", "wout")]
        wT = [sb(f"{n}T", [EH, 2, E]) for n in ("wq", "wk", "wv")]
        woutT_a = sb("woutT_a", [EA, E])
        woutT_b = sb("woutT_b", [EB, E])
        BROWS = EXPERTS * HT + 4
        QA, QB, KA, KB = range(EXPERTS * HT, BROWS)
        bias_rows = sb("bias_rows", [BROWS, P])
        bias_cols = sb("bias_cols", [P, BROWS])
        bout_bc = sb("bout_bc", [P, E])
        bv_bc = sb("bv_bc", [P, E])
        br_bc = sb("br_bc", [P, EXPERTS])
        b2_sb = sb("b2_sb", [EXPERTS, E])
        wr_a = sb("wr_a", [EA, EXPERTS])
        wr_b = sb("wr_b", [EB, EXPERTS])
        head_of_row2 = sb("head_of_row2", [P, 2, HG])
        head_of_row = sb("head_of_row", [P, HG])
        head_of_block = sb("head_of_block", [P, HG])
        eps = sb("eps", [P, 1])
        expert_no = sb("expert_no", [P, EXPERTS])
        h_tok = sb("h_tok", [P, NP, E])
        h_bout = sb("h_bout", [P, NP, E])
        hT = sb("hT", [EH, 2, TOKENS])
        row_max = sb("row_max", [P, GROUPS, PATCHES])
        row_sum = sb("row_sum", [P, GROUPS, PATCHES])
        row_inv = sb("row_inv", [P, GROUPS, PATCHES])
        attnT_a = sb("attnT_a", [EA, TOKENS])
        attnT_b = sb("attnT_b", [EB, TOKENS])
        y1 = sb("y1", [P, NP, E])
        stats = sb("stats", [P, NP, 6])
        mv = sb("mv", [P, NP, 2])
        std = sb("std", [P, NP])
        rstd = sb("rstd", [P, NP])
        x1 = sb("x1", [P, NP, E])
        x1_tail = sb("x1_tail", [P, NP, 2, EB])
        xa = sb("xa", [P, TOKENS])
        xb = sb("xb", [P, TOKENS])
        xa_hi = sb("xa_hi", [P, TOKENS], F32R)
        xa_lo = sb("xa_lo", [P, TOKENS], F32R)
        xb_hi = sb("xb_hi", [P, TOKENS], F32R)
        xb_lo = sb("xb_lo", [P, TOKENS], F32R)
        logit = sb("logit", [P, NP, EXPERTS])
        lmax = sb("lmax", [P, NP])
        lshift = sb("lshift", [P, NP, EXPERTS])
        lexp = sb("lexp", [P, NP, EXPERTS])
        lsum = sb("lsum", [P, NP])
        linv = sb("linv", [P, NP])
        top = sb("top", [P, NP, 8])
        top_at = sb("top_at", [P, NP, 8], U32)
        top_no = sb("top_no", [P, NP, 8])
        first = sb("first", [P, NP, EXPERTS])
        chosen = sb("chosen", [P, NP, EXPERTS])
        gate_u = sb("gate_u", [P, NP, EXPERTS])
        gate = sb("gate", [P, NP, EXPERTS])
        gateT = sb("gateT", [EXPERTS, TOKENS])
        raw1 = [sb(f"raw1_{i}", [P, 2 * HID]) for i in range(2)]
        raw2 = [sb(f"raw2_{i}", [P, HT, E]) for i in range(2)]
        w1_hi = [sb(f"w1_hi{i}", [P, 2 * HID], F32R) for i in range(2)]
        w1_lo = [sb(f"w1_lo{i}", [P, HID], F32R) for i in range(2)]
        w2_s = [sb(f"w2_s{i}", [P, HT, 2, E], F32R) for i in range(2)]
        acc = sb("acc", [P, NP, 2, E])
        y2 = sb("y2", [P, NP, E])
        y_out = sb("y_out", [P, NP, E])

        def stage(scope):
            return lambda name, shape: scope.enter_context(nc.sbuf_tensor(name, shape, F32))

        with ExitStack() as embedding:
            of = stage(embedding)
            xin = of("xin", [P, PATCH * NP * RUN])
            x_pack = of("x_pack", [P, NP, PATCH_DIM])
            xT = of("xT", [P, KC, TOKENS])
            tokw_sb = of("tokw_sb", [P, KC, E])
        with ExitStack() as attention:
            of = stage(attention)
            q_exp_a = of("q_exp_a", [P, PATCHES, HG, IMGS])
            q_exp_b = of("q_exp_b", [P, PATCHES // 2, HG, IMGS])
            v_rep = of("v_rep", [P, PATCHES, E])
            v_exp = of("v_exp", [P, PATCHES, E])
            shifted = of("shifted", [P, GROUPS, TOKENS])
            expd = of("expd", [P, GROUPS, TOKENS])
            prob = of("prob", [P, GROUPS, TOKENS])
            probT = of("probT", [P, GROUPS, TOKENS])
            k_a = of("k_a", [P, TOKENS])
            k_b = of("k_b", [P, HALF])
            v_tok = of("v_tok", [P, NP, E])
        RAW = 3
        h_raw = [sb(f"h_raw{i}", [P, TOKENS]) for i in range(RAW)]
        h_hi = [sb(f"h_hi{i}", [P, HT, TOKENS], F32R) for i in range(2)]
        h_lo = [sb(f"h_lo{i}", [P, HT, TOKENS], F32R) for i in range(2)]

        x_in = sem("x_in")
        bias_in = sem("bias_in")
        w_in = [sem(f"w_in{i}") for i in range(4)]
        tokw_in = sem("tokw_in")
        pos_in = sem("pos_in")
        small_in = sem("small_in")
        raw1_in = [sem(f"raw1_in{i}") for i in range(2)]
        raw2_in = [sem(f"raw2_in{i}") for i in range(2)]
        out_done = sem("out_done")
        pool_step = sem("pool_step")
        ident_ready = sem("ident_ready")
        pos_sel_ready = sem("pos_sel_ready")
        masks_ready = sem("masks_ready")
        repeat_ready = sem("repeat_ready")
        tp_full = sem("tp_full")
        tp_act = sem("tp_act")
        tp_dve = sem("tp_dve")
        pack_ready = sem("pack_ready")
        h_done = sem("h_done")
        h_act = sem("h_act")
        h_dve = sem("h_dve")
        hb_ready = sem("hb_ready")
        qk_done = sem("qk_done")
        v_done = sem("v_done")
        q_a_ready = sem("q_a_ready")
        kq_ready = sem("kq_ready")
        v_ready = sem("v_ready")
        vrep_done = sem("vrep_done")
        vrep_act = sem("vrep_act")
        vexp_dve = sem("vexp_dve")
        vexp_pool = sem("vexp_pool")
        score_done = sem("score_done")
        smax = sem("smax")
        ssub = sem("ssub")
        sexp = sem("sexp")
        ssum = sem("ssum")
        sinv = sem("sinv")
        prob_ready = sem("prob_ready")
        probT_ready = sem("probT_ready")
        attn_done = sem("attn_done")
        attnT_ready = sem("attnT_ready")
        proj_done = sem("proj_done")
        ln = sem("ln")
        ln_std = sem("ln_std")
        x1_ready = sem("x1_ready")
        x1T_done = sem("x1T_done")
        xa_act = sem("xa_act")
        xb_dve = sem("xb_dve")
        xlo_ready = sem("xlo_ready")
        logit_done = sem("logit_done")
        rt = sem("rt")
        rt_exp = sem("rt_exp")
        gate_ready = sem("gate_ready")
        gateT_done = sem("gateT_done")
        gateT_ready = sem("gateT_ready")
        w1_hi_ready = sem("w1_hi_ready")
        w1_lo_ready = sem("w1_lo_ready")
        w2_hi_ready = sem("w2_hi_ready")
        w2_lo_ready = sem("w2_lo_ready")
        s1_done = sem("s1_done")
        gelu_done = sem("gelu_done")
        h_lo_ready = sem("h_lo_ready")
        s2_done = sem("s2_done")
        acc_ready = sem("acc_ready")
        y2_ready = sem("y2_ready")
        out_ready = sem("out_ready")

        x_src = x.rearrange("b (hp i) w c -> hp b (i w c)", hp=NP)
        x_runs = xin[:, :].rearrange("p (i wp r) -> p wp i r", i=PATCH, wp=NP)
        x_pack_runs = x_pack[:, :, :].rearrange("p wp (i r) -> p wp i r", i=PATCH)
        x_chunk = x_pack[:, :, :].rearrange("p wp (s c) -> p wp c s", c=KC)
        out_dst = out.rearrange("b (hp wp) e -> wp hp b e", hp=NP)
        w2_src = w2.rearrange("e (t p) d -> e p t d", p=P)
        pos_sel_v = pos_sel[:, :, :, :].rearrange("k w h b -> k w (h b)")

        T_WQ, T_WK, T_WV, T_WOUT, T_BIAS, T_X, T_H = 0, 1, 2, 3, 4, 5, 5 + KC

        def wait_item_slot(pe, n):
            if n >= 4:
                pe.wait_ge(tp_dve if n % 2 else tp_act, (n - 4) // 2 + 1)

        def tile_bank(t, par):
            return (t + 2 * par) % 4

        ORDER = [("up", 0), ("up", 1), ("down", 0), ("up", 2), ("down", 1), ("up", 3), ("up", 4),
                 ("down", 2), ("up", 5), ("down", 3)]

        def slot_of(a):
            wp, hp = divmod(a, NP)
            return 2 * (hp + NP * (wp // 2)) + wp % 2

        block = ctx.enter_context(nc.Block())

        @block.sync
        def _(sp):
            for hp in range(NP):
                sp.dma_start(xin[IMGS * hp:IMGS * (hp + 1), :], x_src[hp]).then_inc(x_in, 16)

            sp.dma_start(tokw_sb[:, :, :], tok_w.rearrange("(p c) e -> p c e", c=KC)) \
                .then_inc(tokw_in, 16)

            def load_w1(e, slot):
                sp.dma_start(raw1[slot][:, W1A], w1[e, 0:EA, :]).then_inc(raw1_in[slot], 16)
                for half in range(2):
                    sp.dma_start(raw1[slot][EB * half:EB * (half + 1), W1B], w1[e, EA:E, :]) \
                        .then_inc(raw1_in[slot], 16)

            def load_w2(e, slot):
                sp.dma_start(raw2[slot][:, :, :], w2_src[e]).then_inc(raw2_in[slot], 16)

            sp.wait_ge(x_in, 16 * NP)
            for e in range(2):
                load_w1(e, e)
                load_w2(e, e)
            with sp.Fori(0, (EXPERTS - 2) // 2) as i:
                for j in range(2):
                    e = i * 2 + j
                    sp.wait_ge(w1_lo_ready, i * 4 + 2 * (j + 1))
                    load_w1(e + 2, j)
                    sp.wait_ge(w2_lo_ready, i * 2 + (j + 1))
                    load_w2(e + 2, j)
            for wp in range(NP):
                sp.wait_ge(out_ready, wp + 1)
                for hp in range(NP):
                    sp.dma_start(out_dst[wp, hp], y_out[IMGS * hp:IMGS * (hp + 1), wp, :]) \
                        .then_inc(out_done, 16)
            sp.wait_ge(out_done, 16 * NP * NP)

        @block.gpsimd
        def _(pool):
            steps = [0]

            def chain(ins):
                steps[0] += 1
                ins.then_inc(pool_step, 1)
                pool.wait_ge(pool_step, steps[0])

            chain(nc.gpsimd.memset(ident[:, :], 0.0))
            nc.gpsimd.affine_select(out=ident[:, :], in_=ident[:, :], compare_op=ALU.not_equal,
                                    fill=1.0, base=0, pattern=[[-1, P]],
                                    channel_multiplier=1).then_inc(ident_ready, 1)
            pool.dma_start(pos_sb[0:PATCHES, :], pos).then_inc(pos_in, 16)
            pool.dma_start(pos_sb[PATCHES:PATCHES + 1, :], tok_b.unsqueeze(0)).then_inc(pos_in, 16)
            chain(nc.gpsimd.memset(pos_sel[:, :, :, :], 0.0))
            chain(nc.gpsimd.affine_select(out=pos_sel[:, :, :, :], in_=pos_sel[:, :, :, :],
                                          compare_op=ALU.not_equal, fill=1.0, base=0,
                                          pattern=[[-1, NP], [-NP, NP], [0, IMGS]],
                                          channel_multiplier=1))
            nc.gpsimd.affine_select(out=pos_sel[:, :, :, :], in_=pos_sel[:, :, :, :],
                                    compare_op=ALU.not_equal, fill=1.0, base=-PATCHES,
                                    pattern=[[0, NP], [0, NP], [0, IMGS]],
                                    channel_multiplier=1).then_inc(pos_sel_ready, 1)
            chain(nc.gpsimd.memset(head_of_row2[:, :, :], 1.0))
            chain(nc.gpsimd.affine_select(out=head_of_row2[:, :, :], in_=head_of_row2[:, :, :],
                                          compare_op=ALU.is_ge, fill=0.0, base=0,
                                          pattern=[[-GE, 2], [-HD, HG]], channel_multiplier=1))
            chain(nc.gpsimd.affine_select(out=head_of_row2[:, :, :], in_=head_of_row2[:, :, :],
                                          compare_op=ALU.is_ge, fill=0.0, base=HD - 1,
                                          pattern=[[GE, 2], [HD, HG]], channel_multiplier=-1))
            chain(nc.gpsimd.tensor_tensor(head_of_row[:, :], head_of_row2[:, 0, :],
                                          head_of_row2[:, 1, :], ALU.add))
            chain(nc.gpsimd.memset(head_of_block[:, :], 1.0))
            chain(nc.gpsimd.affine_select(out=head_of_block[:, :], in_=head_of_block[:, :],
                                          compare_op=ALU.is_ge, fill=0.0, base=0,
                                          pattern=[[-IMGS, HG]], channel_multiplier=1))
            chain(nc.gpsimd.affine_select(out=head_of_block[:, :], in_=head_of_block[:, :],
                                          compare_op=ALU.is_ge, fill=0.0, base=IMGS - 1,
                                          pattern=[[IMGS, HG]], channel_multiplier=-1))
            chain(nc.gpsimd.iota(expert_no[:, :], pattern=[[1, EXPERTS]], base=0,
                                 channel_multiplier=0, allow_small_or_imprecise_dtypes=True))
            nc.gpsimd.memset(eps[:, :], LN_EPS).then_inc(masks_ready, 1)
            pool.dma_start(bv_bc[:, :], bv.partition_broadcast(P)).then_inc(small_in, 16)
            pool.dma_start(bout_bc[:, :], bout.partition_broadcast(P)).then_inc(small_in, 16)
            pool.dma_start(br_bc[:, :], br.partition_broadcast(P)).then_inc(small_in, 16)
            pool.dma_start(b2_sb[:, :], b2).then_inc(small_in, 16)
            pool.dma_start(wr_a[:, :], wr[0:EA, :]).then_inc(small_in, 16)
            pool.dma_start(wr_b[:, :], wr[EA:E, :]).then_inc(small_in, 16)

            def split_w1(slot, e):
                pool.wait_ge(w1_hi_ready, e + 1)
                nc.gpsimd.tensor_tensor(w1_lo[slot][:, :], raw1[slot][:, W1A],
                                        w1_hi[slot][:, W1A].bitcast(F32), ALU.subtract) \
                    .then_inc(w1_lo_ready, 1)
                pool.wait_ge(w1_lo_ready, e * 2 + 1)
                tail = w1_hi[slot][EB:P, W1B]
                nc.gpsimd.tensor_tensor(tail, raw1[slot][EB:P, W1B], tail.bitcast(F32),
                                        ALU.subtract).then_inc(w1_lo_ready, 1)
                pool.wait_ge(w1_lo_ready, e * 2 + 2)

            def split_w2(slot, e):
                pool.wait_ge(w2_hi_ready, e + 1)
                nc.gpsimd.tensor_tensor(w2_s[slot][:, :, 1, :], raw2[slot][:, :, :],
                                        w2_s[slot][:, :, 0, :].bitcast(F32), ALU.subtract) \
                    .then_inc(w2_lo_ready, 1)

            pool.wait_ge(small_in, 16 * 6)
            pool.wait_ge(h_act, 2)
            pool.wait_ge(h_dve, 2)
            nc.gpsimd.tensor_tensor(h_bout[:, :, :], h_tok[:, :, :],
                                    bout_bc[:, :].unsqueeze(1).broadcast_to([P, NP, E]),
                                    ALU.add).then_inc(hb_ready, 1)
            split_w1(0, 0)
            for pair in range(1, PATCHES // 2, 2):
                pool.wait_ge(vrep_act, pair // 2 + 1)
                pg = slice(2 * pair, 2 * pair + 2)
                nc.gpsimd.tensor_tensor(
                    v_exp[:, pg, :].rearrange("p a (g h d) -> p (a g) h d", h=HG, d=HD),
                    v_rep[:, pg, :].rearrange("p a (g h d) -> p (a g) h d", h=HG, d=HD),
                    head_of_block[:, :].unsqueeze(1).unsqueeze(3)
                    .broadcast_to([P, 2 * GROUPS, HG, HD]), ALU.mult).then_inc(vexp_pool, 1)
            for g in range(GROUPS):
                pool.wait_ge(sinv, g + 1)
                nc.gpsimd.tensor_tensor(
                    prob[:, g, :].rearrange("p (a k) -> p a k", k=IMGS),
                    expd[:, g, :].rearrange("p (a k) -> p a k", k=IMGS),
                    row_inv[:, g, :].unsqueeze(2).broadcast_to([P, PATCHES, IMGS]),
                    ALU.mult).then_inc(prob_ready, 1)
            split_w1(1, 1)
            split_w2(0, 0)
            with pool.Fori(0, (EXPERTS - 2) // 2) as i:
                for j in range(2):
                    split_w1(j, i * 2 + (j + 2))
                    split_w2(1 - j, i * 2 + (j + 1))
            split_w2(1, EXPERTS - 1)

        @block.scalar
        def _(act):
            for n, w in enumerate((wq, wk, wv, wout)):
                act.dma_start(w_nat[n][:, :, :], w.rearrange("(c p) e -> p c e", p=EH)) \
                    .then_inc(w_in[n], 16)
            act.dma_start(bias_rows[0:EXPERTS * HT, :],
                          b1.rearrange("e (t p) -> (e t) p", p=P)).then_inc(bias_in, 16)
            for row, src in ((QA, bq), (KA, bk)):
                src = src.unsqueeze(0)
                act.dma_start(bias_rows[row:row + 1, :], src[:, 0:EA]).then_inc(bias_in, 16)
                act.dma_start(bias_rows[row + 1:row + 2, :].rearrange("p (a e) -> p a e", a=2),
                              src[:, EA:E].unsqueeze(1).broadcast_to([1, 2, EB])) \
                    .then_inc(bias_in, 16)

            def take_item(n, pairs):
                act.wait_ge(tp_full, n + 1)
                for dst, src in pairs[:-1]:
                    nc.scalar.copy(dst, src)
                nc.scalar.copy(*pairs[-1]).then_inc(tp_act, 1)

            for n, w in ((T_WQ, 0), (T_WV, 2)):
                take_item(n, [(wT[w][:, :, :].rearrange("p c e -> p (c e)"),
                               bank[n][0:EH, 0:2 * E])])
            take_item(T_BIAS, [(bias_cols[:, :], bank[0][:, 0:BROWS])])
            act.wait_ge(x_in, 16 * NP)
            nc.scalar.copy(x_pack_runs[:, 3], x_runs[:, 3]).then_inc(pack_ready, 1)
            for c in range(1, KC, 2):
                take_item(T_X + c, [(xT[:, c, :], bank[(T_X + c) % 4][:, :])])
            for wp in range(2):
                act.wait_ge(h_done, wp + 1)
                nc.scalar.copy(h_tok[:, wp, :], bank[4 + wp][:, 0:E]).then_inc(h_act, 1)
            take_item(T_H + 1, [(hT[:, 1, :], bank[(T_H + 1) % 4][0:EH, :])])
            act.wait_ge(masks_ready, 1)
            act.wait_ge(qk_done, 2)
            nc.scalar.activation(k_a[:, :], bank[1][:, :], ACT.Identity,
                                 bias=bias_cols[:, KA:KA + 1]).then_inc(kq_ready, 1)
            act.wait_ge(qk_done, 4)
            nc.scalar.activation(k_b[:, :], bank[3][:, 0:HALF], ACT.Identity,
                                 bias=bias_cols[:, KB:KB + 1]).then_inc(kq_ready, 1)
            def copy_vrep(pair):
                act.wait_ge(vrep_done, pair + 1)
                nc.scalar.copy(v_rep[:, 2 * pair:2 * pair + 2, :].rearrange("p a e -> p (a e)"),
                               bank[4 + pair % 4][:, 0:2 * E]).then_inc(vrep_act, 1)

            copy_vrep(1)
            copy_vrep(3)
            for g in range(GROUPS):
                act.wait_ge(ssub, g + 1)
                nc.scalar.activation(expd[:, g, :], shifted[:, g, :], ACT.Exp,
                                     scale=SCALE).then_inc(sexp, 1)
                if g < 2:
                    copy_vrep(2 * g + 5)
            act.wait_ge(attn_done, 1)
            nc.scalar.copy(attnT_a[:, :], bank[0][:, :]).then_inc(attnT_ready, 1)
            act.wait_ge(ln, 2 * NP)
            nc.scalar.activation(std[:, :], mv[:, :, 1], ACT.Sqrt, bias=eps[:, 0:1]).then_inc(ln_std, 1)
            act.wait_ge(x1T_done, 1)
            nc.scalar.copy(xa[:, :], bank[0][:, :]).then_inc(xa_act, 1)
            nc.scalar.copy(xa_hi[:, :], bank[0][:, :]).then_inc(xa_act, 1)
            act.wait_ge(rt, 3)
            nc.scalar.activation(lexp[:, :, :], lshift[:, :, :], ACT.Exp).then_inc(rt_exp, 1)

            def gelu(tile, n, b1_col, par, h_free):
                act.wait_ge(s1_done, n + 1)
                bias = bias_cols[:, bass.ds(b1_col, 1)]
                src = bank[tile_bank(tile, par)][:, :]
                if h_free is not None:
                    h_free()
                nc.scalar.activation(h_raw[tile % RAW][:, :], src, ACT.Gelu, bias=bias) \
                    .then_inc(gelu_done, 1)
                nc.scalar.activation(h_hi[par][:, tile, :], src, ACT.Gelu, bias=bias) \
                    .then_inc(gelu_done, 1)

            for t in range(HT):
                def free(t=t):
                    if t >= RAW:
                        act.wait_ge(h_lo_ready, t - RAW + 1)
                gelu(t, t, t, 0, free)

            def up_step(e, par_next):
                for t in range(HT):
                    n = e * HT + (HT + t)

                    def free(t=t, n=n):
                        act.wait_ge(h_lo_ready, n - (RAW - 1))
                        if t == 0:
                            act.wait_ge(s2_done, e * NP + NP)
                    gelu(t, n, n, par_next, free)

            with act.Fori(0, (EXPERTS - 2) // 2) as i:
                for j in range(2):
                    up_step(i * 2 + j, 1 - j)
            up_step(EXPERTS - 2, 1)
            for wp in range(NP):
                act.wait_ge(ln, 2 * NP + 2 * (wp + 1))
                nc.scalar.activation(std[:, wp:wp + 1], mv[:, wp, 1:2], ACT.Sqrt,
                                     bias=eps[:, 0:1]).then_inc(ln_std, 1)

        @block.vector
        def _(dve):
            def take_item(n, dst, src):
                dve.wait_ge(tp_full, n + 1)
                nc.vector.tensor_copy(dst, src).then_inc(tp_dve, 1)

            nc.vector.memset(acc[:, :, :, :], 0.0).then_inc(rt, 1)
            dve.wait_ge(ident_ready, 1)
            for b in range(NP):
                rows = slice(IMGS * b, IMGS * (b + 1))
                nc.vector.tensor_copy(repeat[rows, :, :], ident[rows, rows].unsqueeze(1)
                                      .broadcast_to([IMGS, HG, IMGS])).then_inc(repeat_ready, 1)
            take_item(T_WK, wT[1][:, :, :].rearrange("p c e -> p (c e)"), bank[1][0:EH, 0:2 * E])
            dve.wait_ge(tp_full, T_WOUT + 1)
            nc.vector.tensor_copy(woutT_b[:, :], bank[3][0:EB, E:2 * E])
            take_item(T_WOUT, woutT_a[:, :], bank[3][:, 0:E])
            dve.wait_ge(x_in, 16 * NP)
            for wp in range(3):
                nc.vector.tensor_copy(x_pack_runs[:, wp], x_runs[:, wp]).then_inc(pack_ready, 1)
            for c in range(0, KC, 2):
                take_item(T_X + c, xT[:, c, :], bank[(T_X + c) % 4][:, :])
            for wp in range(2, NP):
                dve.wait_ge(h_done, wp + 1)
                nc.vector.tensor_copy(h_tok[:, wp, :], bank[4 + wp][:, 0:E]).then_inc(h_dve, 1)
            take_item(T_H, hT[:, 0, :], bank[T_H % 4][0:EH, :])

            dve.wait_ge(masks_ready, 1)
            dve.wait_ge(tp_act, T_BIAS // 2 + 1)

            def expand_q(dst, src, col):
                for h in range(HG):
                    ins = nc.vector.tensor_scalar(dst[:, :, h, :], src,
                                                  bias_cols[:, col:col + 1],
                                                  head_of_row[:, h:h + 1], ALU.add, ALU.mult)
                ins.then_inc(q_a_ready, 1)

            dve.wait_ge(qk_done, 1)
            expand_q(q_exp_a, bank[0][:, :].rearrange("p (a q) -> p a q", q=IMGS), QA)
            dve.wait_ge(qk_done, 3)
            expand_q(q_exp_b, bank[2][:, 0:HALF].rearrange("p (a q) -> p a q", q=IMGS), QB)
            dve.wait_ge(small_in, 16 * 6)
            for wp in range(NP):
                dve.wait_ge(v_done, wp + 1)
                nc.vector.tensor_tensor(v_tok[:, wp, :], bank[4 + wp][:, 0:E], bv_bc[:, :],
                                        ALU.add).then_inc(v_ready, 1)

            def hi_w1(slot, landed):
                dve.wait_ge(raw1_in[slot], landed)
                nc.vector.tensor_copy(w1_hi[slot][:, :], raw1[slot][:, :]).then_inc(w1_hi_ready, 1)

            def hi_w2(slot, landed):
                dve.wait_ge(raw2_in[slot], landed)
                nc.vector.tensor_copy(w2_s[slot][:, :, 0, :], raw2[slot][:, :, :]) \
                    .then_inc(w2_hi_ready, 1)

            hi_w1(0, 48)

            def mask_v(pair):
                dve.wait_ge(vrep_done, pair + 1)
                nc.vector.tensor_tensor(
                    v_exp[:, 2 * pair:2 * pair + 2, :]
                    .rearrange("p a (g h d) -> p (a g) h d", h=HG, d=HD),
                    bank[4 + pair % 4][:, 0:2 * E].rearrange("p (g h d) -> p g h d", h=HG, d=HD),
                    head_of_block[:, :].unsqueeze(1).unsqueeze(3)
                    .broadcast_to([P, 2 * GROUPS, HG, HD]), ALU.mult).then_inc(vexp_dve, 1)

            HP_ = PATCHES // 2
            parts = [[(0, 0, PATCHES)], [(1, 0, PATCHES)], [(2, 0, HP_), (3, HP_, PATCHES)]]

            def shift(g):
                dve.wait_ge(score_done, g + 1)
                for b, lo, hi in parts[g]:
                    ins = nc.vector.tensor_reduce(
                        row_max[:, g, lo:hi],
                        bank[b][:, 0:(hi - lo) * IMGS].rearrange("p (a k) -> p a k", k=IMGS),
                        AX, ALU.max)
                ins.then_inc(smax, 1)
                dve.wait_ge(smax, g + 1)
                for b, lo, hi in parts[g]:
                    ins = nc.vector.tensor_tensor(
                        shifted[:, g, lo * IMGS:hi * IMGS].rearrange("p (a k) -> p a k", k=IMGS),
                        bank[b][:, 0:(hi - lo) * IMGS].rearrange("p (a k) -> p a k", k=IMGS),
                        row_max[:, g, lo:hi].unsqueeze(2).broadcast_to([P, hi - lo, IMGS]),
                        ALU.subtract)
                ins.then_inc(ssub, 1)

            def invert(g):
                dve.wait_ge(sexp, g + 1)
                nc.vector.tensor_reduce(row_sum[:, g, :],
                                        expd[:, g, :].rearrange("p (a k) -> p a k", k=IMGS),
                                        AX, ALU.add).then_inc(ssum, 1)
                dve.wait_ge(ssum, g + 1)
                nc.vector.reciprocal(row_inv[:, g, :], row_sum[:, g, :]).then_inc(sinv, 1)

            def turn(g):
                dve.wait_ge(prob_ready, g + 1)
                nc.vector.transpose(probT[:, g, :], prob[:, g, :]).then_inc(probT_ready, 1)

            shift(0)
            mask_v(0)
            shift(1)
            invert(0)
            mask_v(2)
            shift(2)
            invert(1)
            mask_v(4)
            turn(0)
            invert(2)
            mask_v(6)
            turn(1)
            hi_w1(1, 48)
            turn(2)
            hi_w2(0, 16)
            dve.wait_ge(attn_done, 2)
            nc.vector.tensor_copy(attnT_b[:, :], bank[1][0:EB, :]).then_inc(attnT_ready, 1)

            ln_count = [0]

            def ln_step(ins):
                ln_count[0] += 1
                ins.then_inc(ln, 1)

            dve.wait_ge(hb_ready, 1)
            for wp in range(NP):
                dve.wait_ge(proj_done, wp + 1)
                nc.vector.tensor_tensor(y1[:, wp, :], bank[4 + wp][:, 0:E], h_bout[:, wp, :],
                                        ALU.add).then_inc(x1_ready, 1)
            for wp in range(NP):
                dve.wait_ge(x1_ready, wp + 1)
                ln_step(nc.vector.bn_stats(stats[:, wp, :], y1[:, wp, :]))
            for wp in range(NP):
                dve.wait_ge(ln, wp + 1)
                ln_step(nc.vector.bn_aggr(mv[:, wp, :], stats[:, wp, :]))
            dve.wait_ge(ln_std, 1)
            nc.vector.reciprocal(rstd[:, :], std[:, :]).then_inc(x1_ready, 1)
            dve.wait_ge(x1_ready, NP + 1)
            for wp in range(NP):
                nc.vector.tensor_scalar(x1[:, wp, :], y1[:, wp, :], mv[:, wp, 0:1],
                                        rstd[:, wp:wp + 1], ALU.subtract, ALU.mult) \
                    .then_inc(x1_ready, 1)
            for wp in range(NP):
                nc.vector.tensor_scalar(x1_tail[:, wp, :, :],
                                        y1[:, wp, EA:E].unsqueeze(1).broadcast_to([P, 2, EB]),
                                        mv[:, wp, 0:1], rstd[:, wp:wp + 1], ALU.subtract,
                                        ALU.mult).then_inc(x1_ready, 1)
            dve.wait_ge(x1T_done, 2)
            nc.vector.tensor_copy(xb[:, :], bank[1][:, :]).then_inc(xb_dve, 1)
            nc.vector.tensor_copy(xb_hi[:, :], bank[1][:, :]).then_inc(xb_dve, 1)
            dve.wait_ge(xa_act, 2)
            nc.vector.tensor_tensor(xa_lo[:, :], xa[:, :], xa_hi[:, :].bitcast(F32),
                                    ALU.subtract).then_inc(xlo_ready, 1)
            dve.wait_ge(xb_dve, 2)
            nc.vector.tensor_tensor(xb_lo[:, :], xb[:, :], xb_hi[:, :].bitcast(F32),
                                    ALU.subtract).then_inc(xlo_ready, 1)

            rt_count = [1]

            def rt_step(ins, wait=True):
                rt_count[0] += 1
                ins.then_inc(rt, 1)
                if wait:
                    dve.wait_ge(rt, rt_count[0])

            def by_tile(a):
                return a.unsqueeze(2).broadcast_to([P, NP, EXPERTS])

            dve.wait_ge(logit_done, 1)
            rt_step(nc.vector.tensor_tensor(
                logit[:, :, :], bank[4][:, 0:NP * EXPERTS].rearrange("p (a e) -> p a e", a=NP),
                br_bc[:, :].unsqueeze(1).broadcast_to([P, NP, EXPERTS]), ALU.add))
            nc.vector.tensor_reduce(lmax[:, :], logit[:, :, :], AX, ALU.max).then_inc(x1_ready, 1)
            dve.wait_ge(x1_ready, 3 * NP + 2)
            rt_step(nc.vector.tensor_tensor(lshift[:, :, :], logit[:, :, :], by_tile(lmax[:, :]),
                                            ALU.subtract), wait=False)

            def h_split(t, par, gelus):
                dve.wait_ge(gelu_done, gelus)
                nc.vector.tensor_tensor(h_lo[par][:, t, :], h_raw[t % RAW][:, :],
                                        h_hi[par][:, t, :].bitcast(F32), ALU.subtract) \
                    .then_inc(h_lo_ready, 1)

            dve.wait_ge(rt_exp, 1)
            nc.vector.tensor_reduce(lsum[:, :], lexp[:, :, :], AX, ALU.add).then_inc(rt, 1)
            for wp in range(NP):
                nc.vector.max(top[:, wp, :], lexp[:, wp, :]).then_inc(rt, 1)
            rt_count[0] += 1 + NP
            dve.wait_ge(rt, rt_count[0])
            nc.vector.reciprocal(linv[:, :], lsum[:, :]).then_inc(rt, 1)
            for wp in range(NP):
                nc.vector.max_index(top_at[:, wp, :], top[:, wp, :], lexp[:, wp, :]).then_inc(rt, 1)
            rt_count[0] += 1 + NP
            h_split(0, 0, 2)
            dve.wait_ge(rt, rt_count[0])
            rt_step(nc.vector.tensor_copy(top_no[:, :, :], top_at[:, :, :]))
            for wp in range(NP):
                rt_step(nc.vector.tensor_scalar(first[:, wp, :], expert_no[:, :],
                                                top_no[:, wp, 0:1], None, ALU.is_equal), wait=False)
            h_split(1, 0, 4)
            dve.wait_ge(rt, rt_count[0])
            for wp in range(NP):
                rt_step(nc.vector.scalar_tensor_tensor(
                    out=chosen[:, wp, :], in0=expert_no[:, :], scalar=top_no[:, wp, 1:2],
                    in1=first[:, wp, :], op0=ALU.is_equal, op1=ALU.add), wait=False)
            dve.wait_ge(rt, rt_count[0])
            rt_step(nc.vector.tensor_tensor(gate_u[:, :, :], lexp[:, :, :], chosen[:, :, :],
                                            ALU.mult))
            nc.vector.tensor_tensor(gate[:, :, :], gate_u[:, :, :], by_tile(linv[:, :]),
                                    ALU.mult).then_inc(gate_ready, 1)
            for t in range(2, 5):
                h_split(t, 0, 2 * (t + 1))
            dve.wait_ge(gateT_done, 1)
            nc.vector.tensor_copy(gateT[:, :], bank[5][0:EXPERTS, :]).then_inc(gateT_ready, 1)
            h_split(5, 0, 12)
            for wp in range(NP):
                dve.wait_ge(s2_done, wp + 1)
                nc.vector.tensor_tensor(acc[:, wp, 0, :], bank[4 + wp][:, 0:E], x1[:, wp, :],
                                        ALU.add).then_inc(acc_ready, 1)
            dve.wait_ge(gate_ready, 1)

            def combine(e, wp):
                dve.wait_ge(s2_done, e * NP + (NP + wp + 1))
                dve.wait_ge(acc_ready, e * NP + (wp + 1))
                nc.vector.scalar_tensor_tensor(
                    out=acc[:, wp, :, :].rearrange("p a e -> p (a e)"), in0=bank[4 + wp][:, 0:2 * E],
                    scalar=gate[:, wp, bass.ds(e, 1)],
                    in1=acc[:, wp, :, :].rearrange("p a e -> p (a e)"),
                    op0=ALU.mult, op1=ALU.add).then_inc(acc_ready, 1)

            def step(e, par, landed1, landed2):
                if landed1 is not None:
                    hi_w1(par, landed1)
                hi_w2(1 - par, landed2)
                for kind, k in ORDER:
                    if kind == "up":
                        h_split(k, 1 - par, (e * HT + (HT + k + 1)) * 2)
                    else:
                        combine(e, k)

            with dve.Fori(0, (EXPERTS - 2) // 2) as i:
                step(i * 2, 0, (i + 2) * 48, (i + 1) * 16)
                step(i * 2 + 1, 1, (i + 2) * 48, (i + 2) * 16)
            step(EXPERTS - 2, 0, None, 16 * (EXPERTS // 2))
            for wp in range(NP):
                combine(EXPERTS - 1, wp)
                done = EXPERTS * NP + NP
                dve.wait_ge(acc_ready, EXPERTS * NP + wp + 1)
                nc.vector.tensor_tensor(y2[:, wp, :], acc[:, wp, 0, :], acc[:, wp, 1, :],
                                        ALU.add).then_inc(y2_ready, 1)
                dve.wait_ge(y2_ready, 3 * wp + 1)
                ln_step(nc.vector.bn_stats(stats[:, wp, :], y2[:, wp, :]))
                dve.wait_ge(ln, ln_count[0])
                ln_step(nc.vector.bn_aggr(mv[:, wp, :], stats[:, wp, :]))
                dve.wait_ge(ln_std, wp + 2)
                nc.vector.reciprocal(rstd[:, wp:wp + 1], std[:, wp:wp + 1]).then_inc(y2_ready, 2)
                dve.wait_ge(y2_ready, 3 * wp + 3)
                nc.vector.tensor_scalar(y_out[:, wp, :], y2[:, wp, :], mv[:, wp, 0:1],
                                        rstd[:, wp:wp + 1], ALU.subtract, ALU.mult) \
                    .then_inc(out_ready, 1)

        @block.tensor
        def _(pe):
            def item(n, outs_ins):
                wait_item_slot(pe, n)
                for o, i_ in outs_ins:
                    k = i_.shape[0]
                    mm = pe.transpose(o, i_, ident[0:k, 0:k])
                mm.then_inc(tp_full, 1)

            pe.wait_ge(ident_ready, 1)
            for n, w in ((T_WQ, 0), (T_WK, 1), (T_WV, 2)):
                pe.wait_ge(w_in[w], 16)
                item(n, [(bank[n % 4][0:EH, E * ci + EH * co:E * ci + EH * (co + 1)],
                          w_nat[w][:, co, EH * ci:EH * (ci + 1)]) for ci in range(2) for co in range(2)])
            pe.wait_ge(w_in[3], 16)
            item(T_WOUT, [(bank[T_WOUT % 4][0:n_in, E * ci + EH * co:E * ci + EH * (co + 1)],
                           w_nat[3][:, co, at:at + n_in])
                          for ci, (at, n_in) in enumerate(((0, EA), (EA, EB))) for co in range(2)])
            pe.wait_ge(bias_in, 16 * 5)
            item(T_BIAS, [(bank[T_BIAS % 4][:, 0:BROWS], bias_rows[:, :])])
            pe.wait_ge(pos_sel_ready, 1)
            pe.wait_ge(pos_in, 32)
            for wp in range(NP):
                pe.matmul(bank[4 + wp][:, 0:E], pos_sel_v[:, wp, :], pos_sb[:, :],
                          start=True, stop=False)
            pe.wait_ge(pack_ready, NP)
            pe.wait_ge(tokw_in, 16)

            def embed(c):
                n = T_X + c
                pe.wait_ge(tp_dve if n % 2 else tp_act, n // 2 + 1)
                for wp in range(NP):
                    mm = pe.matmul(bank[4 + wp][:, 0:E], xT[:, c, P * wp:P * (wp + 1)],
                                   tokw_sb[:, c, :], start=False, stop=(c == KC - 1))
                    if c == KC - 1:
                        mm.then_inc(h_done, 1)

            for c in range(KC):
                n = T_X + c
                item(n, [(bank[n % 4][:, P * wp:P * (wp + 1)], x_chunk[:, wp, c])
                         for wp in range(NP)])
                if c:
                    embed(c - 1)
            embed(KC - 1)
            pe.wait_ge(h_act, 2)
            pe.wait_ge(h_dve, 2)
            for ci in range(2):
                n = T_H + ci
                item(n, [(bank[n % 4][0:EH, P * wp:P * (wp + 1)],
                          h_tok[:, wp, EH * ci:EH * (ci + 1)]) for wp in range(NP)])
            pe.wait_ge(tp_dve, T_H // 2 + 1)
            pe.wait_ge(tp_act, (T_H + 1) // 2 + 1)
            for n, w in ((0, 0), (1, 1)):
                for ci in range(2):
                    mm = pe.matmul(bank[n][:, :], wT[w][:, ci, 0:EA], hT[:, ci, :],
                                   start=(ci == 0), stop=(ci == 1))
                mm.then_inc(qk_done, 1)
            for n, w in ((2, 0), (3, 1)):
                for half in range(2):
                    for ci in range(2):
                        mm = pe.matmul(bank[n][EB * half:EB * (half + 1), 0:HALF],
                                       wT[w][:, ci, EA:E], hT[:, ci, HALF * half:HALF * (half + 1)],
                                       start=(ci == 0), stop=(ci == 1))
                mm.then_inc(qk_done, 1)
            for wp in range(NP):
                for ci in range(2):
                    mm = pe.matmul(bank[4 + wp][:, 0:E], hT[:, ci, P * wp:P * (wp + 1)],
                                   wT[2][:, ci, :], start=(ci == 0), stop=(ci == 1))
                mm.then_inc(v_done, 1)
            pe.wait_ge(q_a_ready, 1)
            pe.wait_ge(kq_ready, 1)
            for g in range(2):
                rows = slice(GE * g, GE * (g + 1))
                for a in range(PATCHES):
                    mm = pe.matmul(bank[g][:, IMGS * a:IMGS * (a + 1)],
                                   q_exp_a[rows, a, :, :].rearrange("p h q -> p (h q)"),
                                   k_a[rows, IMGS * a:IMGS * (a + 1)], start=True, stop=True)
                mm.then_inc(score_done, 1)
            pe.wait_ge(q_a_ready, 2)
            pe.wait_ge(kq_ready, 2)
            for half in range(2):
                rows = slice(EB * half, EB * (half + 1))
                for a in range(PATCHES // 2):
                    mm = pe.matmul(bank[2 + half][:, IMGS * a:IMGS * (a + 1)],
                                   q_exp_b[rows, a, :, :].rearrange("p h q -> p (h q)"),
                                   k_b[rows, IMGS * a:IMGS * (a + 1)], start=True, stop=True)
            mm.then_inc(score_done, 1)
            pe.wait_ge(v_ready, NP)
            pe.wait_ge(repeat_ready, NP)
            for pair in range(PATCHES // 2):
                if pair >= 4:
                    prev = pair - 4
                    if prev % 2:
                        pe.wait_ge(vrep_act, prev // 2 + 1)
                    else:
                        pe.wait_ge(vexp_dve, prev // 2 + 1)
                for k in range(2):
                    wp, hp = 2 * (pair // NP) + k, pair % NP
                    rows = slice(IMGS * hp, IMGS * (hp + 1))
                    mm = pe.matmul(bank[4 + pair % 4][:, E * k:E * (k + 1)],
                                   repeat[rows, :, :].rearrange("p h k -> p (h k)"),
                                   v_tok[rows, wp, :], start=True, stop=True)
                mm.then_inc(vrep_done, 1)
            pe.wait_ge(vexp_dve, 4)
            pe.wait_ge(vexp_pool, 4)
            for g in range(GROUPS):
                pe.wait_ge(probT_ready, g + 1)
                dst = bank[g // 2][GE * (g % 2):GE * (g % 2 + 1), :]
                for a in range(PATCHES):
                    mm = pe.matmul(dst[:, IMGS * a:IMGS * (a + 1)],
                                   v_exp[:, slot_of(a), GE * g:GE * (g + 1)],
                                   probT[:, g, IMGS * a:IMGS * (a + 1)], start=True, stop=True)
                if g > 0:
                    mm.then_inc(attn_done, 1)
            pe.wait_ge(attnT_ready, 2)
            for wp in range(NP):
                tok = slice(P * wp, P * (wp + 1))
                pe.matmul(bank[4 + wp][:, 0:E], attnT_a[:, tok], woutT_a[:, :], start=True, stop=False)
                pe.matmul(bank[4 + wp][:, 0:E], attnT_b[:, tok], woutT_b[:, :], start=False, stop=True) \
                    .then_inc(proj_done, 1)
            for b in range(2):
                for wp in range(NP):
                    pe.wait_ge(x1_ready, NP + 2 + NP * b + wp)
                    src = x1_tail[:, wp, :, :].rearrange("p a e -> p (a e)") if b else \
                        x1[:, wp, 0:EA]
                    mm = pe.transpose(bank[b][:, P * wp:P * (wp + 1)], src, ident[:, :])
                mm.then_inc(x1T_done, 1)
            def router_logits():
                for wp in range(NP):
                    tok = slice(P * wp, P * (wp + 1))
                    dst = bank[4][:, EXPERTS * wp:EXPERTS * (wp + 1)]
                    pe.matmul(dst, xa[:, tok], wr_a[:, :], start=True, stop=False)
                    mm = pe.matmul(dst, xb[0:EB, tok], wr_b[:, :], start=False, stop=True)
                mm.then_inc(logit_done, 1)

            def up(t, par, first=False):
                b = bank[tile_bank(t, par)][:, :]
                cols = slice(P * t, P * (t + 1))
                tail = slice(HID + P * t, HID + P * (t + 1))
                pe.matmul(b, w1_hi[par][:, cols], xa_hi[:, :], start=True, stop=False)
                pe.matmul(b, w1_lo[par][:, cols], xa_hi[:, :], start=False, stop=False)
                pe.matmul(b, w1_hi[par][:, tail], xb_hi[:, :], start=False, stop=False)
                if first:
                    pe.wait_ge(xlo_ready, 2)
                pe.matmul(b, w1_hi[par][:, cols], xa_lo[:, :], start=False, stop=False)
                pe.matmul(b, w1_hi[par][:, tail], xb_lo[:, :], start=False, stop=True) \
                    .then_inc(s1_done, 1)

            def down(wp, par):
                tok = slice(P * wp, P * (wp + 1))

                def hi(t, start=False, stop=False):
                    return pe.matmul(bank[4 + wp][:, 0:2 * E], h_hi[par][:, t, tok],
                                     w2_s[par][:, t, :, :].rearrange("p a e -> p (a e)"),
                                     start=start, stop=stop, skip_group_check=True)

                hi(0, start=True)
                for t in range(HT):
                    pe.matmul(bank[4 + wp][:, 0:E], h_lo[par][:, t, tok], w2_s[par][:, t, 0, :],
                              start=False, stop=False, skip_group_check=True)
                    if t > 0:
                        mm = hi(t, stop=(t == HT - 1))
                mm.then_inc(s2_done, 1)

            pe.wait_ge(xa_act, 2)
            pe.wait_ge(xb_dve, 2)
            pe.wait_ge(w1_lo_ready, 2)
            for t in range(HT):
                if t >= 4:
                    pe.wait_ge(gelu_done, 2 * (t - 4 + 1))
                up(t, 0, first=(t == 0))
                if t == 0:
                    router_logits()
                if t == 4:
                    pe.wait_ge(gate_ready, 1)
                    for wp in range(NP):
                        mm = pe.matmul(bank[5][0:EXPERTS, P * wp:P * (wp + 1)], gate[:, wp, :],
                                       ident[:, :], start=True, stop=True)
                    mm.then_inc(gateT_done, 1)
            pe.wait_ge(gateT_ready, 1)
            for wp in range(NP):
                pe.matmul(bank[4 + wp][:, 0:E], gateT[:, P * wp:P * (wp + 1)], b2_sb[:, :],
                          start=True, stop=True).then_inc(s2_done, 1)

            def step(e, par):
                for kind, k in ORDER:
                    if kind == "up":
                        if k == 0:
                            pe.wait_ge(w1_lo_ready, e * 2 + 4)
                        pe.wait_ge(gelu_done, (e * HT + (HT + k - 3)) * 2)
                        up(k, 1 - par)
                    else:
                        if k == 0:
                            pe.wait_ge(w2_lo_ready, e + 1)
                            pe.wait_ge(h_lo_ready, e * HT + HT)
                        pe.wait_ge(acc_ready, e * NP + (k + 1))
                        down(k, par)

            with pe.Fori(0, (EXPERTS - 2) // 2) as i:
                step(i * 2, 0)
                step(i * 2 + 1, 1)
            step(EXPERTS - 2, 0)
            pe.wait_ge(w2_lo_ready, EXPERTS)
            pe.wait_ge(h_lo_ready, EXPERTS * HT)
            for wp in range(NP):
                pe.wait_ge(acc_ready, (EXPERTS - 1) * NP + wp + 1)
                down(wp, 1)


_INS = ["x", "L0_tok_W", "L0_tok_b", "L0_tok_pos_emb", "L0_attn_Wq", "L0_attn_bq", "L0_attn_Wk",
        "L0_attn_bk", "L0_attn_Wv", "L0_attn_bv", "L0_attn_Wout", "L0_attn_bout", "L0_ffn_W1",
        "L0_ffn_b1", "L0_ffn_W2", "L0_ffn_b2", "L0_ffn_Wr", "L0_ffn_br"]


def kernel(**inputs):
    import numpy as np
    import concourse.bacc as bacc
    from concourse.bass_utils import run_bass_kernel_spmd

    nc = bacc.Bacc("TRN2", target_bir_lowering=False, num_devices=1)
    arrays, args = {}, []
    for name in _INS:
        a = np.ascontiguousarray(inputs[name])
        arrays[f"in_{name}_dram"] = a
        args.append(nc.dram_tensor(f"in_{name}_dram", a.shape, mybir.dt.from_np(a.dtype),
                                   kind="ExternalInput").ap())
    images, side = inputs["x"].shape[0], inputs["x"].shape[1]
    shape = (images, (side // PATCH) ** 2, inputs["L0_tok_W"].shape[1])
    out = nc.dram_tensor("out_0_dram", shape, F32, kind="ExternalOutput").ap()
    build(nc, *args, out)
    r = run_bass_kernel_spmd(nc, [arrays], core_ids=[0])
    return r.results[0]["out_0_dram"]
```

```python
from contextlib import ExitStack

import concourse.bass as bass
from concourse import mybir

F32 = mybir.dt.float32
F32R = mybir.dt.float32r
U32 = mybir.dt.uint32
ALU = mybir.AluOpType
ACT = mybir.ActivationFunctionType
AX = mybir.AxisListType.X

P = 128
PATCH = 16
CHANNELS = 3
HEADS = 12
TOP_K = 2
LN_EPS = 1e-5
BANK = 512


def build(nc, x, tok_w, tok_b, pos, wq, bq, wk, bk, wv, bv, wout, bout, w1, b1, w2, b2, wr, br, out):
    IMGS, SIDE = x.shape[0], x.shape[1]
    E = tok_w.shape[1]
    NP = SIDE // PATCH
    PATCHES = NP * NP
    TOKENS = IMGS * PATCHES
    PATCH_DIM = PATCH * PATCH * CHANNELS
    RUN = PATCH * CHANNELS
    KC = PATCH_DIM // P
    HD = E // HEADS
    EH = E // 2
    PAIR = 2 * HD
    RT = P // PAIR
    EA, EB = P, E - P
    EXPERTS, HID = w1.shape[0], w1.shape[2]
    HT = HID // P
    HALF = TOKENS // 2
    SCALE = float(HD) ** -0.5
    AS = NP * 2 * IMGS
    BS = AS // 2
    SC = AS + BS
    SLOTS = SC // IMGS
    assert NP * IMGS == P and KC * P == PATCH_DIM and 2 * EB == P and PAIR == IMGS and RT == NP
    assert HEADS * HD == E and EB == 2 * PAIR
    assert EXPERTS == 8 and TOKENS == BANK and NP == 4 and HT == 6

    W1A, W1B = slice(0, HID), slice(HID, 2 * HID)

    with ExitStack() as ctx:
        def sb(name, shape, dt=F32):
            return ctx.enter_context(nc.sbuf_tensor(name, shape, dt))

        def sem(name):
            return ctx.enter_context(nc.semaphore(name))

        low = ctx.enter_context(nc.psum_tensor("banks_0_3", [P, 4, BANK], F32))
        high = ctx.enter_context(nc.psum_tensor("banks_4_7", [P, 4, BANK], F32))
        bank = [(low if i < 4 else high)[:, i % 4, :] for i in range(8)]

        ident = sb("ident", [P, P])
        pos_sb = sb("pos_sb", [PATCHES + 1, E])
        pos_sel = sb("pos_sel", [PATCHES + 1, NP, NP, IMGS])
        w_nat = [sb(f"{n}_nat", [EH, 2, E]) for n in ("wq", "wk", "wv", "wout")]
        wT = [sb(f"{n}T", [EH, 2, E]) for n in ("wq", "wk", "wv")]
        woutT_a = sb("woutT_a", [EA, E])
        woutT_b = sb("woutT_b", [P, E])
        BROWS = EXPERTS * HT + 4
        QA, QB, KA, KB = range(EXPERTS * HT, BROWS)
        bias_rows = sb("bias_rows", [BROWS, P])
        bias_cols = sb("bias_cols", [P, BROWS])
        bout_bc = sb("bout_bc", [P, E])
        bv_bc = sb("bv_bc", [P, E])
        br_bc = sb("br_bc", [P, EXPERTS])
        b2_sb = sb("b2_sb", [EXPERTS, E])
        wr_a = sb("wr_a", [EA, EXPERTS])
        wr_b = sb("wr_b", [EB, EXPERTS])
        in_block = sb("in_block", [P, RT, 2])
        in_block2 = sb("in_block2", [P, 2, 2])
        is_head = sb("is_head", [P, 2])
        is_head_b = sb("is_head_b", [P, 1])
        eps = sb("eps", [P, 1])
        expert_no = sb("expert_no", [P, EXPERTS])
        h_tok = sb("h_tok", [P, NP, E])
        h_bout = sb("h_bout", [P, NP, E])
        hT = sb("hT", [EH, 2, TOKENS])
        row_max = sb("row_max", [P, RT, SLOTS])
        row_sum = sb("row_sum", [P, RT, SLOTS])
        row_inv = sb("row_inv", [P, RT, SLOTS])
        attnT_a = sb("attnT_a", [EA, TOKENS])
        attnT_b = sb("attnT_b", [P, TOKENS])
        y1 = sb("y1", [P, NP, E])
        stats = sb("stats", [P, NP, 6])
        mv = sb("mv", [P, NP, 2])
        std = sb("std", [P, NP])
        rstd = sb("rstd", [P, NP])
        x1 = sb("x1", [P, NP, E])
        x1_tail = sb("x1_tail", [P, NP, 2, EB])
        xa = sb("xa", [P, TOKENS])
        xb = sb("xb", [P, TOKENS])
        xa_hi = sb("xa_hi", [P, TOKENS], F32R)
        xa_lo = sb("xa_lo", [P, TOKENS], F32R)
        xb_hi = sb("xb_hi", [P, TOKENS], F32R)
        xb_lo = sb("xb_lo", [P, TOKENS], F32R)
        logit = sb("logit", [P, NP, EXPERTS])
        lmax = sb("lmax", [P, NP])
        lshift = sb("lshift", [P, NP, EXPERTS])
        lexp = sb("lexp", [P, NP, EXPERTS])
        lsum = sb("lsum", [P, NP])
        linv = sb("linv", [P, NP])
        top = sb("top", [P, NP, 8])
        top_at = sb("top_at", [P, NP, 8], U32)
        top_no = sb("top_no", [P, NP, 8])
        first = sb("first", [P, NP, EXPERTS])
        chosen = sb("chosen", [P, NP, EXPERTS])
        gate_u = sb("gate_u", [P, NP, EXPERTS])
        gate = sb("gate", [P, NP, EXPERTS])
        gateT = sb("gateT", [EXPERTS, TOKENS])
        raw1 = [sb(f"raw1_{i}", [P, 2 * HID]) for i in range(2)]
        raw2 = [sb(f"raw2_{i}", [P, HT, E]) for i in range(2)]
        w1_hi = [sb(f"w1_hi{i}", [P, 2 * HID], F32R) for i in range(2)]
        w1_lo = [sb(f"w1_lo{i}", [P, HID], F32R) for i in range(2)]
        w2_s = [sb(f"w2_s{i}", [P, HT, 2, E], F32R) for i in range(2)]
        acc = sb("acc", [P, NP, 2, E])
        y2 = sb("y2", [P, NP, E])
        y_out = sb("y_out", [P, NP, E])

        def stage(scope):
            return lambda name, shape: scope.enter_context(nc.sbuf_tensor(name, shape, F32))

        with ExitStack() as embedding:
            of = stage(embedding)
            xin = of("xin", [P, PATCH * NP * RUN])
            x_pack = of("x_pack", [P, NP, PATCH_DIM])
            xT = of("xT", [P, KC, TOKENS])
            tokw_sb = of("tokw_sb", [P, KC, E])
        with ExitStack() as attention:
            of = stage(attention)
            q_a = of("q_a", [P, TOKENS])
            q_b = of("q_b", [P, HALF])
            k_exp_a = of("k_exp_a", [P, PATCHES, 2, IMGS])
            k_exp_b = of("k_exp_b", [P, PATCHES // 2, 2, IMGS])
            shifted = of("shifted", [P, RT, SC])
            expd = of("expd", [P, RT, SC])
            prob = of("prob", [P, RT, SC])
            probT = of("probT", [P, RT, SC])
            attn_first = of("attn_first", [P, TOKENS])
            v_raw = of("v_raw", [P, NP, E])
            v_tok = of("v_tok", [P, NP, E])
        RAW = 3
        h_raw = [sb(f"h_raw{i}", [P, TOKENS]) for i in range(RAW)]
        h_hi = [sb(f"h_hi{i}", [P, HT, TOKENS], F32R) for i in range(2)]
        h_lo = [sb(f"h_lo{i}", [P, HT, TOKENS], F32R) for i in range(2)]

        x_in = sem("x_in")
        bias_in = sem("bias_in")
        w_in = [sem(f"w_in{i}") for i in range(4)]
        tokw_in = sem("tokw_in")
        pos_in = sem("pos_in")
        small_in = sem("small_in")
        raw1_in = [sem(f"raw1_in{i}") for i in range(2)]
        raw2_in = [sem(f"raw2_in{i}") for i in range(2)]
        out_done = sem("out_done")
        pool_step = sem("pool_step")
        ident_ready = sem("ident_ready")
        pos_sel_ready = sem("pos_sel_ready")
        masks_ready = sem("masks_ready")
        tp_full = sem("tp_full")
        tp_act = sem("tp_act")
        tp_dve = sem("tp_dve")
        pack_ready = sem("pack_ready")
        h_done = sem("h_done")
        h_act = sem("h_act")
        h_dve = sem("h_dve")
        hb_ready = sem("hb_ready")
        qk_done = sem("qk_done")
        v_done = sem("v_done")
        q_ready = sem("q_ready")
        k_ready = sem("k_ready")
        v_raw_ready = sem("v_raw_ready")
        v_ready = sem("v_ready")
        score_done = sem("score_done")
        smax = sem("smax")
        ssub = sem("ssub")
        sexp = sem("sexp")
        ssum = sem("ssum")
        sinv = sem("sinv")
        prob_ready = sem("prob_ready")
        probT_ready = sem("probT_ready")
        attn_done = sem("attn_done")
        attn_step = sem("attn_step")
        attnT_ready = sem("attnT_ready")
        attnT_b_ready = sem("attnT_b_ready")
        proj_done = sem("proj_done")
        ln = sem("ln")
        ln_std = sem("ln_std")
        x1_ready = sem("x1_ready")
        x1T_done = sem("x1T_done")
        xa_act = sem("xa_act")
        xb_dve = sem("xb_dve")
        xlo_ready = sem("xlo_ready")
        logit_done = sem("logit_done")
        rt = sem("rt")
        rt_exp = sem("rt_exp")
        gate_ready = sem("gate_ready")
        gateT_done = sem("gateT_done")
        gateT_ready = sem("gateT_ready")
        w1_hi_ready = sem("w1_hi_ready")
        w1_lo_ready = sem("w1_lo_ready")
        w2_hi_ready = sem("w2_hi_ready")
        w2_lo_ready = sem("w2_lo_ready")
        s1_done = sem("s1_done")
        gelu_done = sem("gelu_done")
        h_lo_ready = sem("h_lo_ready")
        s2_done = sem("s2_done")
        acc_ready = sem("acc_ready")
        y2_ready = sem("y2_ready")
        out_ready = sem("out_ready")

        x_src = x.rearrange("b (hp i) w c -> hp b (i w c)", hp=NP)
        x_runs = xin[:, :].rearrange("p (i wp r) -> p wp i r", i=PATCH, wp=NP)
        x_pack_runs = x_pack[:, :, :].rearrange("p wp (i r) -> p wp i r", i=PATCH)
        x_chunk = x_pack[:, :, :].rearrange("p wp (s c) -> p wp c s", c=KC)
        out_dst = out.rearrange("b (hp wp) e -> wp hp b e", hp=NP)
        w2_src = w2.rearrange("e (t p) d -> e p t d", p=P)
        pos_sel_v = pos_sel[:, :, :, :].rearrange("k w h b -> k w (h b)")

        T_WQ, T_WK, T_WV, T_WOUT, T_BIAS, T_X, T_H = 0, 1, 2, 3, 4, 5, 5 + KC

        def wait_item_slot(pe, n):
            if n >= 4:
                pe.wait_ge(tp_dve if n % 2 else tp_act, (n - 4) // 2 + 1)

        def tile_bank(t, par):
            return (t + 2 * par) % 4

        ORDER = [("up", 0), ("up", 1), ("down", 0), ("up", 2), ("down", 1), ("up", 3), ("up", 4),
                 ("down", 2), ("up", 5), ("down", 3)]

        def by_patch(a):
            return a[:, :].rearrange("p (wp hp q) -> p hp wp q", wp=NP, hp=NP)

        block = ctx.enter_context(nc.Block())

        @block.sync
        def _(sp):
            for hp in range(NP):
                sp.dma_start(xin[IMGS * hp:IMGS * (hp + 1), :], x_src[hp]).then_inc(x_in, 16)

            sp.dma_start(tokw_sb[:, :, :], tok_w.rearrange("(p c) e -> p c e", c=KC)) \
                .then_inc(tokw_in, 16)

            def load_w1(e, slot):
                sp.dma_start(raw1[slot][:, W1A], w1[e, 0:EA, :]).then_inc(raw1_in[slot], 16)
                for half in range(2):
                    sp.dma_start(raw1[slot][EB * half:EB * (half + 1), W1B], w1[e, EA:E, :]) \
                        .then_inc(raw1_in[slot], 16)

            def load_w2(e, slot):
                sp.dma_start(raw2[slot][:, :, :], w2_src[e]).then_inc(raw2_in[slot], 16)

            sp.wait_ge(x_in, 16 * NP)
            for e in range(2):
                load_w1(e, e)
                load_w2(e, e)
            with sp.Fori(0, (EXPERTS - 2) // 2) as i:
                for j in range(2):
                    e = i * 2 + j
                    sp.wait_ge(w1_lo_ready, i * 4 + 2 * (j + 1))
                    load_w1(e + 2, j)
                    sp.wait_ge(w2_lo_ready, i * 2 + (j + 1))
                    load_w2(e + 2, j)
            for wp in range(NP):
                sp.wait_ge(out_ready, wp + 1)
                for hp in range(NP):
                    sp.dma_start(out_dst[wp, hp], y_out[IMGS * hp:IMGS * (hp + 1), wp, :]) \
                        .then_inc(out_done, 16)
            sp.wait_ge(out_done, 16 * NP * NP)

        @block.gpsimd
        def _(pool):
            steps = [0]

            def chain(ins):
                steps[0] += 1
                ins.then_inc(pool_step, 1)
                pool.wait_ge(pool_step, steps[0])

            chain(nc.gpsimd.memset(ident[:, :], 0.0))
            nc.gpsimd.affine_select(out=ident[:, :], in_=ident[:, :], compare_op=ALU.not_equal,
                                    fill=1.0, base=0, pattern=[[-1, P]],
                                    channel_multiplier=1).then_inc(ident_ready, 1)
            pool.dma_start(pos_sb[0:PATCHES, :], pos).then_inc(pos_in, 16)
            pool.dma_start(pos_sb[PATCHES:PATCHES + 1, :], tok_b.unsqueeze(0)).then_inc(pos_in, 16)
            chain(nc.gpsimd.memset(pos_sel[:, :, :, :], 0.0))
            chain(nc.gpsimd.affine_select(out=pos_sel[:, :, :, :], in_=pos_sel[:, :, :, :],
                                          compare_op=ALU.not_equal, fill=1.0, base=0,
                                          pattern=[[-1, NP], [-NP, NP], [0, IMGS]],
                                          channel_multiplier=1))
            nc.gpsimd.affine_select(out=pos_sel[:, :, :, :], in_=pos_sel[:, :, :, :],
                                    compare_op=ALU.not_equal, fill=1.0, base=-PATCHES,
                                    pattern=[[0, NP], [0, NP], [0, IMGS]],
                                    channel_multiplier=1).then_inc(pos_sel_ready, 1)
            chain(nc.gpsimd.memset(in_block[:, :, :], 1.0))
            chain(nc.gpsimd.affine_select(out=in_block[:, :, :], in_=in_block[:, :, :],
                                          compare_op=ALU.is_ge, fill=0.0, base=0,
                                          pattern=[[-PAIR, RT], [-HD, 2]], channel_multiplier=1))
            chain(nc.gpsimd.affine_select(out=in_block[:, :, :], in_=in_block[:, :, :],
                                          compare_op=ALU.is_ge, fill=0.0, base=HD - 1,
                                          pattern=[[PAIR, RT], [HD, 2]], channel_multiplier=-1))
            chain(nc.gpsimd.tensor_tensor(in_block2[:, :, :], in_block[:, 0:2, :],
                                          in_block[:, 2:4, :], ALU.add))
            chain(nc.gpsimd.tensor_tensor(is_head[:, :], in_block2[:, 0, :], in_block2[:, 1, :],
                                          ALU.add))
            chain(nc.gpsimd.iota(expert_no[:, :], pattern=[[1, EXPERTS]], base=0,
                                 channel_multiplier=0, allow_small_or_imprecise_dtypes=True))
            nc.gpsimd.memset(eps[:, :], LN_EPS).then_inc(masks_ready, 1)
            pool.dma_start(bv_bc[:, :], bv.partition_broadcast(P)).then_inc(small_in, 16)
            pool.dma_start(bout_bc[:, :], bout.partition_broadcast(P)).then_inc(small_in, 16)
            pool.dma_start(br_bc[:, :], br.partition_broadcast(P)).then_inc(small_in, 16)
            pool.dma_start(b2_sb[:, :], b2).then_inc(small_in, 16)
            pool.dma_start(wr_a[:, :], wr[0:EA, :]).then_inc(small_in, 16)
            pool.dma_start(wr_b[:, :], wr[EA:E, :]).then_inc(small_in, 16)

            def split_w1(slot, e):
                pool.wait_ge(w1_hi_ready, e + 1)
                nc.gpsimd.tensor_tensor(w1_lo[slot][:, :], raw1[slot][:, W1A],
                                        w1_hi[slot][:, W1A].bitcast(F32), ALU.subtract) \
                    .then_inc(w1_lo_ready, 1)
                pool.wait_ge(w1_lo_ready, e * 2 + 1)
                tail = w1_hi[slot][EB:P, W1B]
                nc.gpsimd.tensor_tensor(tail, raw1[slot][EB:P, W1B], tail.bitcast(F32),
                                        ALU.subtract).then_inc(w1_lo_ready, 1)
                pool.wait_ge(w1_lo_ready, e * 2 + 2)

            def split_w2(slot, e):
                pool.wait_ge(w2_hi_ready, e + 1)
                nc.gpsimd.tensor_tensor(w2_s[slot][:, :, 1, :], raw2[slot][:, :, :],
                                        w2_s[slot][:, :, 0, :].bitcast(F32), ALU.subtract) \
                    .then_inc(w2_lo_ready, 1)

            pool.wait_ge(small_in, 16 * 6)
            pool.wait_ge(h_act, 2)
            pool.wait_ge(h_dve, 2)
            nc.gpsimd.tensor_tensor(h_bout[:, :, :], h_tok[:, :, :],
                                    bout_bc[:, :].unsqueeze(1).broadcast_to([P, NP, E]),
                                    ALU.add).then_inc(hb_ready, 1)
            split_w1(0, 0)
            pool.wait_ge(v_raw_ready, NP)
            nc.gpsimd.tensor_tensor(v_tok[:, :, :], v_raw[:, :, :],
                                    bv_bc[:, :].unsqueeze(1).broadcast_to([P, NP, E]),
                                    ALU.add).then_inc(v_ready, 1)
            for r in range(RT):
                pool.wait_ge(sinv, r + 1)
                nc.gpsimd.tensor_tensor(
                    prob[:, r, :].rearrange("p (a k) -> p a k", k=IMGS),
                    expd[:, r, :].rearrange("p (a k) -> p a k", k=IMGS),
                    row_inv[:, r, :].unsqueeze(2).broadcast_to([P, SLOTS, IMGS]),
                    ALU.mult).then_inc(prob_ready, 1)
            split_w1(1, 1)
            split_w2(0, 0)
            with pool.Fori(0, (EXPERTS - 2) // 2) as i:
                for j in range(2):
                    split_w1(j, i * 2 + (j + 2))
                    split_w2(1 - j, i * 2 + (j + 1))
            split_w2(1, EXPERTS - 1)

        @block.scalar
        def _(act):
            for n, w in enumerate((wq, wk, wv, wout)):
                act.dma_start(w_nat[n][:, :, :], w.rearrange("(c p) e -> p c e", p=EH)) \
                    .then_inc(w_in[n], 16)
            act.dma_start(bias_rows[0:EXPERTS * HT, :],
                          b1.rearrange("e (t p) -> (e t) p", p=P)).then_inc(bias_in, 16)
            for row, src in ((QA, bq), (KA, bk)):
                src = src.unsqueeze(0)
                act.dma_start(bias_rows[row:row + 1, :], src[:, 0:EA]).then_inc(bias_in, 16)
                act.dma_start(bias_rows[row + 1:row + 2, :].rearrange("p (a e) -> p a e", a=2),
                              src[:, EA:E].unsqueeze(1).broadcast_to([1, 2, EB])) \
                    .then_inc(bias_in, 16)

            def take_item(n, pairs):
                act.wait_ge(tp_full, n + 1)
                for dst, src in pairs[:-1]:
                    nc.scalar.copy(dst, src)
                nc.scalar.copy(*pairs[-1]).then_inc(tp_act, 1)

            for n, w in ((T_WQ, 0), (T_WV, 2)):
                take_item(n, [(wT[w][:, :, :].rearrange("p c e -> p (c e)"),
                               bank[n][0:EH, 0:2 * E])])
            take_item(T_BIAS, [(bias_cols[:, :], bank[0][:, 0:BROWS])])
            act.wait_ge(x_in, 16 * NP)
            nc.scalar.copy(x_pack_runs[:, 3], x_runs[:, 3]).then_inc(pack_ready, 1)
            for c in range(1, KC, 2):
                take_item(T_X + c, [(xT[:, c, :], bank[(T_X + c) % 4][:, :])])
            for wp in range(2):
                act.wait_ge(h_done, wp + 1)
                nc.scalar.copy(h_tok[:, wp, :], bank[4 + wp][:, 0:E]).then_inc(h_act, 1)
            take_item(T_H + 1, [(hT[:, 1, :], bank[(T_H + 1) % 4][0:EH, :])])
            act.wait_ge(qk_done, 1)
            nc.scalar.activation(q_a[:, :], bank[0], ACT.Identity,
                                 bias=bias_cols[:, QA:QA + 1]).then_inc(q_ready, 1)
            act.wait_ge(qk_done, 3)
            nc.scalar.activation(q_b[:, :], bank[2][:, 0:HALF], ACT.Identity,
                                 bias=bias_cols[:, QB:QB + 1]).then_inc(q_ready, 1)
            for wp in range(NP):
                act.wait_ge(v_done, wp + 1)
                nc.scalar.copy(v_raw[:, wp, :], bank[4 + wp][:, 0:E]).then_inc(v_raw_ready, 1)
            for r in range(RT):
                act.wait_ge(ssub, r + 1)
                nc.scalar.activation(expd[:, r, :], shifted[:, r, :], ACT.Exp,
                                     scale=SCALE).then_inc(sexp, 1)
            act.wait_ge(attn_done, 1)
            nc.scalar.activation(by_patch(attnT_b), low[:, :, 0:NP * IMGS]
                                 .rearrange("p hp (wp q) -> p hp wp q", q=IMGS), ACT.Copy,
                                 scale=is_head_b[:, 0:1]).then_inc(attnT_b_ready, 1)
            act.wait_ge(ln, 2 * NP)
            nc.scalar.activation(std[:, :], mv[:, :, 1], ACT.Sqrt, bias=eps[:, 0:1]).then_inc(ln_std, 1)
            act.wait_ge(x1T_done, 1)
            nc.scalar.copy(xa[:, :], bank[4]).then_inc(xa_act, 1)
            nc.scalar.copy(xa_hi[:, :], bank[4]).then_inc(xa_act, 1)
            act.wait_ge(rt, 3)
            nc.scalar.activation(lexp[:, :, :], lshift[:, :, :], ACT.Exp).then_inc(rt_exp, 1)

            def gelu(tile, n, b1_col, par, h_free):
                act.wait_ge(s1_done, n + 1)
                bias = bias_cols[:, bass.ds(b1_col, 1)]
                src = bank[tile_bank(tile, par)][:, :]
                if h_free is not None:
                    h_free()
                nc.scalar.activation(h_raw[tile % RAW][:, :], src, ACT.Gelu, bias=bias) \
                    .then_inc(gelu_done, 1)
                nc.scalar.activation(h_hi[par][:, tile, :], src, ACT.Gelu, bias=bias) \
                    .then_inc(gelu_done, 1)

            for t in range(HT):
                def free(t=t):
                    if t >= RAW:
                        act.wait_ge(h_lo_ready, t - RAW + 1)
                gelu(t, t, t, 0, free)

            def up_step(e, par_next):
                for t in range(HT):
                    n = e * HT + (HT + t)

                    def free(t=t, n=n):
                        act.wait_ge(h_lo_ready, n - (RAW - 1))
                        if t == 0:
                            act.wait_ge(s2_done, e * NP + NP)
                    gelu(t, n, n, par_next, free)

            with act.Fori(0, (EXPERTS - 2) // 2) as i:
                for j in range(2):
                    up_step(i * 2 + j, 1 - j)
            up_step(EXPERTS - 2, 1)
            for wp in range(NP):
                act.wait_ge(ln, 2 * NP + 2 * (wp + 1))
                nc.scalar.activation(std[:, wp:wp + 1], mv[:, wp, 1:2], ACT.Sqrt,
                                     bias=eps[:, 0:1]).then_inc(ln_std, 1)

        @block.vector
        def _(dve):
            def take_item(n, dst, src):
                dve.wait_ge(tp_full, n + 1)
                nc.vector.tensor_copy(dst, src).then_inc(tp_dve, 1)

            nc.vector.memset(acc[:, :, :, :], 0.0).then_inc(rt, 1)
            dve.wait_ge(ident_ready, 1)
            take_item(T_WK, wT[1][:, :, :].rearrange("p c e -> p (c e)"), bank[1][0:EH, 0:2 * E])
            dve.wait_ge(tp_full, T_WOUT + 1)
            nc.vector.tensor_copy(woutT_b[:, :], bank[3][:, E:2 * E])
            take_item(T_WOUT, woutT_a[:, :], bank[3][:, 0:E])
            dve.wait_ge(x_in, 16 * NP)
            for wp in range(3):
                nc.vector.tensor_copy(x_pack_runs[:, wp], x_runs[:, wp]).then_inc(pack_ready, 1)
            for c in range(0, KC, 2):
                take_item(T_X + c, xT[:, c, :], bank[(T_X + c) % 4][:, :])
            for wp in range(2, NP):
                dve.wait_ge(h_done, wp + 1)
                nc.vector.tensor_copy(h_tok[:, wp, :], bank[4 + wp][:, 0:E]).then_inc(h_dve, 1)
            take_item(T_H, hT[:, 0, :], bank[T_H % 4][0:EH, :])

            dve.wait_ge(masks_ready, 1)
            nc.vector.tensor_copy(is_head_b[0:EB, :], is_head[0:EB, 0:1]).then_inc(attn_step, 1)
            nc.vector.tensor_copy(is_head_b[EB:P, :], is_head[EB:P, 1:2]).then_inc(attn_step, 1)
            dve.wait_ge(tp_act, T_BIAS // 2 + 1)

            def expand_k(dst, src, col):
                for h in range(2):
                    ins = nc.vector.tensor_scalar(dst[:, :, h, :],
                                                  src.rearrange("p (a k) -> p a k", k=IMGS),
                                                  bias_cols[:, col:col + 1],
                                                  is_head[:, h:h + 1], ALU.add, ALU.mult)
                ins.then_inc(k_ready, 1)

            dve.wait_ge(qk_done, 2)
            expand_k(k_exp_a, bank[1], KA)
            dve.wait_ge(qk_done, 4)
            expand_k(k_exp_b, bank[3][:, 0:HALF], KB)

            def hi_w1(slot, landed):
                dve.wait_ge(raw1_in[slot], landed)
                nc.vector.tensor_copy(w1_hi[slot][:, :], raw1[slot][:, :]).then_inc(w1_hi_ready, 1)

            def hi_w2(slot, landed):
                dve.wait_ge(raw2_in[slot], landed)
                nc.vector.tensor_copy(w2_s[slot][:, :, 0, :], raw2[slot][:, :, :]) \
                    .then_inc(w2_hi_ready, 1)

            hi_w1(0, 48)

            def shift(r):
                scores = bank[r][:, 0:SC].rearrange("p (a k) -> p a k", k=IMGS)
                dve.wait_ge(score_done, r + 1)
                nc.vector.tensor_reduce(row_max[:, r, :], scores, AX, ALU.max).then_inc(smax, 1)
                dve.wait_ge(smax, r + 1)
                nc.vector.tensor_tensor(
                    shifted[:, r, :].rearrange("p (a k) -> p a k", k=IMGS), scores,
                    row_max[:, r, :].unsqueeze(2).broadcast_to([P, SLOTS, IMGS]),
                    ALU.subtract).then_inc(ssub, 1)

            def invert(r):
                dve.wait_ge(sexp, r + 1)
                nc.vector.tensor_reduce(row_sum[:, r, :],
                                        expd[:, r, :].rearrange("p (a k) -> p a k", k=IMGS),
                                        AX, ALU.add).then_inc(ssum, 1)
                dve.wait_ge(ssum, r + 1)
                nc.vector.reciprocal(row_inv[:, r, :], row_sum[:, r, :]).then_inc(sinv, 1)

            def turn(r):
                dve.wait_ge(prob_ready, r + 1)
                nc.vector.transpose(probT[:, r, :], prob[:, r, :]).then_inc(probT_ready, 1)

            shift(0)
            shift(1)
            invert(0)
            shift(2)
            invert(1)
            turn(0)
            shift(3)
            invert(2)
            turn(1)
            invert(3)
            turn(2)
            hi_w1(1, 48)
            turn(3)
            both = high[:, :, 0:AS].rearrange("p hp (wp h q) -> p hp wp h q", h=2, q=IMGS)
            dve.wait_ge(attn_done, 2)
            nc.vector.tensor_scalar(by_patch(attn_first), both[:, :, :, 0, :], is_head[:, 0:1],
                                    None, ALU.mult).then_inc(attn_step, 1)
            dve.wait_ge(attn_step, 3)
            for wp in range(NP):
                nc.vector.scalar_tensor_tensor(
                    out=by_patch(attnT_a)[:, :, wp, :], in0=both[:, :, wp, 1, :],
                    scalar=is_head[:, 1:2], in1=by_patch(attn_first)[:, :, wp, :],
                    op0=ALU.mult, op1=ALU.add).then_inc(attnT_ready, 1)
            hi_w2(0, 16)

            ln_count = [0]

            def ln_step(ins):
                ln_count[0] += 1
                ins.then_inc(ln, 1)

            dve.wait_ge(hb_ready, 1)
            for wp in range(NP):
                dve.wait_ge(proj_done, wp + 1)
                nc.vector.tensor_tensor(y1[:, wp, :], bank[wp][:, 0:E], h_bout[:, wp, :],
                                        ALU.add).then_inc(x1_ready, 1)
            for wp in range(NP):
                dve.wait_ge(x1_ready, wp + 1)
                ln_step(nc.vector.bn_stats(stats[:, wp, :], y1[:, wp, :]))
            for wp in range(NP):
                dve.wait_ge(ln, wp + 1)
                ln_step(nc.vector.bn_aggr(mv[:, wp, :], stats[:, wp, :]))
            dve.wait_ge(ln_std, 1)
            nc.vector.reciprocal(rstd[:, :], std[:, :]).then_inc(x1_ready, 1)
            dve.wait_ge(x1_ready, NP + 1)
            for wp in range(NP):
                nc.vector.tensor_scalar(x1[:, wp, :], y1[:, wp, :], mv[:, wp, 0:1],
                                        rstd[:, wp:wp + 1], ALU.subtract, ALU.mult) \
                    .then_inc(x1_ready, 1)
            for wp in range(NP):
                nc.vector.tensor_scalar(x1_tail[:, wp, :, :],
                                        y1[:, wp, EA:E].unsqueeze(1).broadcast_to([P, 2, EB]),
                                        mv[:, wp, 0:1], rstd[:, wp:wp + 1], ALU.subtract,
                                        ALU.mult).then_inc(x1_ready, 1)
            dve.wait_ge(x1T_done, 2)
            nc.vector.tensor_copy(xb[:, :], bank[5]).then_inc(xb_dve, 1)
            nc.vector.tensor_copy(xb_hi[:, :], bank[5]).then_inc(xb_dve, 1)
            dve.wait_ge(xa_act, 2)
            nc.vector.tensor_tensor(xa_lo[:, :], xa[:, :], xa_hi[:, :].bitcast(F32),
                                    ALU.subtract).then_inc(xlo_ready, 1)
            dve.wait_ge(xb_dve, 2)
            nc.vector.tensor_tensor(xb_lo[:, :], xb[:, :], xb_hi[:, :].bitcast(F32),
                                    ALU.subtract).then_inc(xlo_ready, 1)

            rt_count = [1]

            def rt_step(ins, wait=True):
                rt_count[0] += 1
                ins.then_inc(rt, 1)
                if wait:
                    dve.wait_ge(rt, rt_count[0])

            def by_tile(a):
                return a.unsqueeze(2).broadcast_to([P, NP, EXPERTS])

            dve.wait_ge(logit_done, 1)
            rt_step(nc.vector.tensor_tensor(
                logit[:, :, :], bank[4][:, 0:NP * EXPERTS].rearrange("p (a e) -> p a e", a=NP),
                br_bc[:, :].unsqueeze(1).broadcast_to([P, NP, EXPERTS]), ALU.add))
            nc.vector.tensor_reduce(lmax[:, :], logit[:, :, :], AX, ALU.max).then_inc(x1_ready, 1)
            dve.wait_ge(x1_ready, 3 * NP + 2)
            rt_step(nc.vector.tensor_tensor(lshift[:, :, :], logit[:, :, :], by_tile(lmax[:, :]),
                                            ALU.subtract), wait=False)

            def h_split(t, par, gelus):
                dve.wait_ge(gelu_done, gelus)
                nc.vector.tensor_tensor(h_lo[par][:, t, :], h_raw[t % RAW][:, :],
                                        h_hi[par][:, t, :].bitcast(F32), ALU.subtract) \
                    .then_inc(h_lo_ready, 1)

            dve.wait_ge(rt_exp, 1)
            nc.vector.tensor_reduce(lsum[:, :], lexp[:, :, :], AX, ALU.add).then_inc(rt, 1)
            for wp in range(NP):
                nc.vector.max(top[:, wp, :], lexp[:, wp, :]).then_inc(rt, 1)
            rt_count[0] += 1 + NP
            dve.wait_ge(rt, rt_count[0])
            nc.vector.reciprocal(linv[:, :], lsum[:, :]).then_inc(rt, 1)
            for wp in range(NP):
                nc.vector.max_index(top_at[:, wp, :], top[:, wp, :], lexp[:, wp, :]).then_inc(rt, 1)
            rt_count[0] += 1 + NP
            h_split(0, 0, 2)
            dve.wait_ge(rt, rt_count[0])
            rt_step(nc.vector.tensor_copy(top_no[:, :, :], top_at[:, :, :]))
            for wp in range(NP):
                rt_step(nc.vector.tensor_scalar(first[:, wp, :], expert_no[:, :],
                                                top_no[:, wp, 0:1], None, ALU.is_equal), wait=False)
            h_split(1, 0, 4)
            dve.wait_ge(rt, rt_count[0])
            for wp in range(NP):
                rt_step(nc.vector.scalar_tensor_tensor(
                    out=chosen[:, wp, :], in0=expert_no[:, :], scalar=top_no[:, wp, 1:2],
                    in1=first[:, wp, :], op0=ALU.is_equal, op1=ALU.add), wait=False)
            dve.wait_ge(rt, rt_count[0])
            rt_step(nc.vector.tensor_tensor(gate_u[:, :, :], lexp[:, :, :], chosen[:, :, :],
                                            ALU.mult))
            nc.vector.tensor_tensor(gate[:, :, :], gate_u[:, :, :], by_tile(linv[:, :]),
                                    ALU.mult).then_inc(gate_ready, 1)
            for t in range(2, 5):
                h_split(t, 0, 2 * (t + 1))
            dve.wait_ge(gateT_done, 1)
            nc.vector.tensor_copy(gateT[:, :], bank[5][0:EXPERTS, :]).then_inc(gateT_ready, 1)
            h_split(5, 0, 12)
            for wp in range(NP):
                dve.wait_ge(s2_done, wp + 1)
                nc.vector.tensor_tensor(acc[:, wp, 0, :], bank[4 + wp][:, 0:E], x1[:, wp, :],
                                        ALU.add).then_inc(acc_ready, 1)
            dve.wait_ge(gate_ready, 1)

            def combine(e, wp):
                dve.wait_ge(s2_done, e * NP + (NP + wp + 1))
                dve.wait_ge(acc_ready, e * NP + (wp + 1))
                nc.vector.scalar_tensor_tensor(
                    out=acc[:, wp, :, :].rearrange("p a e -> p (a e)"), in0=bank[4 + wp][:, 0:2 * E],
                    scalar=gate[:, wp, bass.ds(e, 1)],
                    in1=acc[:, wp, :, :].rearrange("p a e -> p (a e)"),
                    op0=ALU.mult, op1=ALU.add).then_inc(acc_ready, 1)

            def step(e, par, landed1, landed2):
                if landed1 is not None:
                    hi_w1(par, landed1)
                hi_w2(1 - par, landed2)
                for kind, k in ORDER:
                    if kind == "up":
                        h_split(k, 1 - par, (e * HT + (HT + k + 1)) * 2)
                    else:
                        combine(e, k)

            with dve.Fori(0, (EXPERTS - 2) // 2) as i:
                step(i * 2, 0, (i + 2) * 48, (i + 1) * 16)
                step(i * 2 + 1, 1, (i + 2) * 48, (i + 2) * 16)
            step(EXPERTS - 2, 0, None, 16 * (EXPERTS // 2))
            for wp in range(NP):
                combine(EXPERTS - 1, wp)
                done = EXPERTS * NP + NP
                dve.wait_ge(acc_ready, EXPERTS * NP + wp + 1)
                nc.vector.tensor_tensor(y2[:, wp, :], acc[:, wp, 0, :], acc[:, wp, 1, :],
                                        ALU.add).then_inc(y2_ready, 1)
                dve.wait_ge(y2_ready, 3 * wp + 1)
                ln_step(nc.vector.bn_stats(stats[:, wp, :], y2[:, wp, :]))
                dve.wait_ge(ln, ln_count[0])
                ln_step(nc.vector.bn_aggr(mv[:, wp, :], stats[:, wp, :]))
                dve.wait_ge(ln_std, wp + 2)
                nc.vector.reciprocal(rstd[:, wp:wp + 1], std[:, wp:wp + 1]).then_inc(y2_ready, 2)
                dve.wait_ge(y2_ready, 3 * wp + 3)
                nc.vector.tensor_scalar(y_out[:, wp, :], y2[:, wp, :], mv[:, wp, 0:1],
                                        rstd[:, wp:wp + 1], ALU.subtract, ALU.mult) \
                    .then_inc(out_ready, 1)

        @block.tensor
        def _(pe):
            def item(n, outs_ins):
                wait_item_slot(pe, n)
                for o, i_ in outs_ins:
                    k = i_.shape[0]
                    mm = pe.transpose(o, i_, ident[0:k, 0:k])
                mm.then_inc(tp_full, 1)

            pe.wait_ge(ident_ready, 1)
            for n, w in ((T_WQ, 0), (T_WK, 1), (T_WV, 2)):
                pe.wait_ge(w_in[w], 16)
                item(n, [(bank[n % 4][0:EH, E * ci + EH * co:E * ci + EH * (co + 1)],
                          w_nat[w][:, co, EH * ci:EH * (ci + 1)]) for ci in range(2) for co in range(2)])
            pe.wait_ge(w_in[3], 16)
            for half in range(2):
                for co in range(2):
                    pe.matmul(bank[T_WOUT % 4][EB * half:EB * (half + 1),
                                               E + EH * co:E + EH * (co + 1)],
                              w_nat[3][:, co, EA:E], ident[0:EH, 0:EH], start=True, stop=True)
            item(T_WOUT, [(bank[T_WOUT % 4][:, EH * co:EH * (co + 1)], w_nat[3][:, co, 0:EA])
                          for co in range(2)])
            pe.wait_ge(bias_in, 16 * 5)
            item(T_BIAS, [(bank[T_BIAS % 4][:, 0:BROWS], bias_rows[:, :])])
            pe.wait_ge(pos_sel_ready, 1)
            pe.wait_ge(pos_in, 32)
            for wp in range(NP):
                pe.matmul(bank[4 + wp][:, 0:E], pos_sel_v[:, wp, :], pos_sb[:, :],
                          start=True, stop=False)
            pe.wait_ge(pack_ready, NP)
            pe.wait_ge(tokw_in, 16)

            def embed(c):
                n = T_X + c
                pe.wait_ge(tp_dve if n % 2 else tp_act, n // 2 + 1)
                for wp in range(NP):
                    mm = pe.matmul(bank[4 + wp][:, 0:E], xT[:, c, P * wp:P * (wp + 1)],
                                   tokw_sb[:, c, :], start=False, stop=(c == KC - 1))
                    if c == KC - 1:
                        mm.then_inc(h_done, 1)

            for c in range(KC):
                n = T_X + c
                item(n, [(bank[n % 4][:, P * wp:P * (wp + 1)], x_chunk[:, wp, c])
                         for wp in range(NP)])
                if c:
                    embed(c - 1)
            embed(KC - 1)
            pe.wait_ge(h_act, 2)
            pe.wait_ge(h_dve, 2)
            for ci in range(2):
                n = T_H + ci
                item(n, [(bank[n % 4][0:EH, P * wp:P * (wp + 1)],
                          h_tok[:, wp, EH * ci:EH * (ci + 1)]) for wp in range(NP)])
            pe.wait_ge(tp_dve, T_H // 2 + 1)
            pe.wait_ge(tp_act, (T_H + 1) // 2 + 1)
            for n, w in ((0, 0), (1, 1)):
                for ci in range(2):
                    mm = pe.matmul(bank[n][:, :], wT[w][:, ci, 0:EA], hT[:, ci, :],
                                   start=(ci == 0), stop=(ci == 1))
                mm.then_inc(qk_done, 1)
            for n, w in ((2, 0), (3, 1)):
                for half in range(2):
                    for ci in range(2):
                        mm = pe.matmul(bank[n][EB * half:EB * (half + 1), 0:HALF],
                                       wT[w][:, ci, EA:E], hT[:, ci, HALF * half:HALF * (half + 1)],
                                       start=(ci == 0), stop=(ci == 1))
                mm.then_inc(qk_done, 1)
            for wp in range(NP):
                for ci in range(2):
                    mm = pe.matmul(bank[4 + wp][:, 0:E], hT[:, ci, P * wp:P * (wp + 1)],
                                   wT[2][:, ci, :], start=(ci == 0), stop=(ci == 1))
                mm.then_inc(v_done, 1)
            pe.wait_ge(q_ready, 2)
            pe.wait_ge(k_ready, 2)
            for r in range(RT):
                rows = slice(PAIR * r, PAIR * (r + 1))
                for wp in range(NP):
                    for hp in range(NP):
                        a = wp * NP + hp
                        pe.matmul(bank[r][IMGS * hp:IMGS * (hp + 1), 2 * IMGS * wp:2 * IMGS * (wp + 1)],
                                  q_a[rows, IMGS * a:IMGS * (a + 1)],
                                  k_exp_a[rows, a, :, :].rearrange("p h k -> p (h k)"),
                                  start=True, stop=True)
                for w in range(NP // 2):
                    for hp in range(NP):
                        a = w * NP + hp
                        at = AS + 2 * IMGS * w
                        mm = pe.matmul(bank[r][IMGS * hp:IMGS * (hp + 1), at:at + 2 * IMGS],
                                       q_b[rows, IMGS * a:IMGS * (a + 1)],
                                       k_exp_b[rows, a, :, :].rearrange("p h k -> p (h k)"),
                                       start=True, stop=True)
                mm.then_inc(score_done, 1)
            pe.wait_ge(v_ready, 1)
            pe.wait_ge(ssub, RT)

            def attend(r):
                pe.wait_ge(probT_ready, r + 1)
                out_rows = slice(PAIR * r, PAIR * (r + 1))
                half, pair = divmod(r, 2)
                for w in range(NP // 2):
                    wp = NP // 2 * half + w
                    for h in range(2):
                        row, at = EB * h + PAIR * pair, AS + IMGS * (2 * w + h)
                        for hp in range(NP):
                            rows = slice(IMGS * hp, IMGS * (hp + 1))
                            last_b = pe.matmul(bank[hp][row:row + PAIR, IMGS * wp:IMGS * (wp + 1)],
                                               v_tok[rows, wp, EA + PAIR * pair:EA + PAIR * (pair + 1)],
                                               probT[rows, r, at:at + IMGS], start=True, stop=True)
                for wp in range(NP):
                    cols = slice(2 * IMGS * wp, 2 * IMGS * (wp + 1))
                    for hp in range(NP):
                        rows = slice(IMGS * hp, IMGS * (hp + 1))
                        last_a = pe.matmul(bank[4 + hp][out_rows, cols],
                                           v_tok[rows, wp, PAIR * r:PAIR * (r + 1)],
                                           probT[rows, r, cols], start=True, stop=True)
                return last_b, last_a

            for r in range(RT):
                last_b, last_a = attend(r)
            last_b.then_inc(attn_done, 1)
            last_a.then_inc(attn_done, 1)
            for wp in range(NP):
                tok = slice(P * wp, P * (wp + 1))
                pe.wait_ge(attnT_ready, wp + 1)
                pe.wait_ge(attnT_b_ready, 1)
                pe.matmul(bank[wp][:, 0:E], attnT_b[:, tok], woutT_b[:, :], start=True, stop=False)
                pe.matmul(bank[wp][:, 0:E], attnT_a[:, tok], woutT_a[:, :], start=False, stop=True) \
                    .then_inc(proj_done, 1)
            for b in range(2):
                for wp in range(NP):
                    pe.wait_ge(x1_ready, NP + 2 + NP * b + wp)
                    src = x1_tail[:, wp, :, :].rearrange("p a e -> p (a e)") if b else \
                        x1[:, wp, 0:EA]
                    mm = pe.transpose(bank[4 + b][:, P * wp:P * (wp + 1)], src, ident[:, :])
                mm.then_inc(x1T_done, 1)
            def router_logits():
                for wp in range(NP):
                    tok = slice(P * wp, P * (wp + 1))
                    dst = bank[4][:, EXPERTS * wp:EXPERTS * (wp + 1)]
                    pe.matmul(dst, xa[:, tok], wr_a[:, :], start=True, stop=False)
                    mm = pe.matmul(dst, xb[0:EB, tok], wr_b[:, :], start=False, stop=True)
                mm.then_inc(logit_done, 1)

            def up(t, par, first=False):
                b = bank[tile_bank(t, par)][:, :]
                cols = slice(P * t, P * (t + 1))
                tail = slice(HID + P * t, HID + P * (t + 1))
                pe.matmul(b, w1_hi[par][:, cols], xa_hi[:, :], start=True, stop=False)
                pe.matmul(b, w1_lo[par][:, cols], xa_hi[:, :], start=False, stop=False)
                pe.matmul(b, w1_hi[par][:, tail], xb_hi[:, :], start=False, stop=False)
                if first:
                    pe.wait_ge(xlo_ready, 2)
                pe.matmul(b, w1_hi[par][:, cols], xa_lo[:, :], start=False, stop=False)
                pe.matmul(b, w1_hi[par][:, tail], xb_lo[:, :], start=False, stop=True) \
                    .then_inc(s1_done, 1)

            def down(wp, par):
                tok = slice(P * wp, P * (wp + 1))

                def hi(t, start=False, stop=False):
                    return pe.matmul(bank[4 + wp][:, 0:2 * E], h_hi[par][:, t, tok],
                                     w2_s[par][:, t, :, :].rearrange("p a e -> p (a e)"),
                                     start=start, stop=stop, skip_group_check=True)

                hi(0, start=True)
                for t in range(HT):
                    pe.matmul(bank[4 + wp][:, 0:E], h_lo[par][:, t, tok], w2_s[par][:, t, 0, :],
                              start=False, stop=False, skip_group_check=True)
                    if t > 0:
                        mm = hi(t, stop=(t == HT - 1))
                mm.then_inc(s2_done, 1)

            pe.wait_ge(xa_act, 2)
            pe.wait_ge(xb_dve, 2)
            pe.wait_ge(w1_lo_ready, 2)
            for t in range(HT):
                if t >= 4:
                    pe.wait_ge(gelu_done, 2 * (t - 4 + 1))
                up(t, 0, first=(t == 0))
                if t == 0:
                    router_logits()
                if t == 4:
                    pe.wait_ge(gate_ready, 1)
                    for wp in range(NP):
                        mm = pe.matmul(bank[5][0:EXPERTS, P * wp:P * (wp + 1)], gate[:, wp, :],
                                       ident[:, :], start=True, stop=True)
                    mm.then_inc(gateT_done, 1)
            pe.wait_ge(gateT_ready, 1)
            for wp in range(NP):
                pe.matmul(bank[4 + wp][:, 0:E], gateT[:, P * wp:P * (wp + 1)], b2_sb[:, :],
                          start=True, stop=True).then_inc(s2_done, 1)

            def step(e, par):
                for kind, k in ORDER:
                    if kind == "up":
                        if k == 0:
                            pe.wait_ge(w1_lo_ready, e * 2 + 4)
                        pe.wait_ge(gelu_done, (e * HT + (HT + k - 3)) * 2)
                        up(k, 1 - par)
                    else:
                        if k == 0:
                            pe.wait_ge(w2_lo_ready, e + 1)
                            pe.wait_ge(h_lo_ready, e * HT + HT)
                        pe.wait_ge(acc_ready, e * NP + (k + 1))
                        down(k, par)

            with pe.Fori(0, (EXPERTS - 2) // 2) as i:
                step(i * 2, 0)
                step(i * 2 + 1, 1)
            step(EXPERTS - 2, 0)
            pe.wait_ge(w2_lo_ready, EXPERTS)
            pe.wait_ge(h_lo_ready, EXPERTS * HT)
            for wp in range(NP):
                pe.wait_ge(acc_ready, (EXPERTS - 1) * NP + wp + 1)
                down(wp, 1)


_INS = ["x", "L0_tok_W", "L0_tok_b", "L0_tok_pos_emb", "L0_attn_Wq", "L0_attn_bq", "L0_attn_Wk",
        "L0_attn_bk", "L0_attn_Wv", "L0_attn_bv", "L0_attn_Wout", "L0_attn_bout", "L0_ffn_W1",
        "L0_ffn_b1", "L0_ffn_W2", "L0_ffn_b2", "L0_ffn_Wr", "L0_ffn_br"]


def kernel(**inputs):
    import numpy as np
    import concourse.bacc as bacc
    from concourse.bass_utils import run_bass_kernel_spmd

    nc = bacc.Bacc("TRN2", target_bir_lowering=False, num_devices=1)
    arrays, args = {}, []
    for name in _INS:
        a = np.ascontiguousarray(inputs[name])
        arrays[f"in_{name}_dram"] = a
        args.append(nc.dram_tensor(f"in_{name}_dram", a.shape, mybir.dt.from_np(a.dtype),
                                   kind="ExternalInput").ap())
    images, side = inputs["x"].shape[0], inputs["x"].shape[1]
    shape = (images, (side // PATCH) ** 2, inputs["L0_tok_W"].shape[1])
    out = nc.dram_tensor("out_0_dram", shape, F32, kind="ExternalOutput").ap()
    build(nc, *args, out)
    r = run_bass_kernel_spmd(nc, [arrays], core_ids=[0])
    return r.results[0]["out_0_dram"]
```

```python
from contextlib import ExitStack

import concourse.bass as bass
from concourse import mybir

F32 = mybir.dt.float32
F32R = mybir.dt.float32r
U32 = mybir.dt.uint32
ALU = mybir.AluOpType
ACT = mybir.ActivationFunctionType
AX = mybir.AxisListType.X

P = 128
PATCH = 16
CHANNELS = 3
HEADS = 12
TOP_K = 2
LN_EPS = 1e-5
BANK = 512
WARM_START = 7
WARM_EXTRACT = 2
WARM_NORM = 4
WARM_COPY = 3


def build(nc, x, tok_w, tok_b, pos, wq, bq, wk, bk, wv, bv, wout, bout, w1, b1, w2, b2, wr, br, out):
    IMGS, SIDE = x.shape[0], x.shape[1]
    E = tok_w.shape[1]
    NP = SIDE // PATCH
    PATCHES = NP * NP
    TOKENS = IMGS * PATCHES
    PATCH_DIM = PATCH * PATCH * CHANNELS
    RUN = PATCH * CHANNELS
    KC = PATCH_DIM // P
    HD = E // HEADS
    EH = E // 2
    PAIR = 2 * HD
    RT = P // PAIR
    EA, EB = P, E - P
    EXPERTS, HID = w1.shape[0], w1.shape[2]
    HT = HID // P
    assert TOP_K == 2
    SCALE = float(HD) ** -0.5
    AS = NP * 2 * IMGS
    SC = [AS, AS, 2 * AS, 2 * AS]
    assert NP * IMGS == P and KC * P == PATCH_DIM and 2 * EB == P and PAIR == IMGS and RT == NP
    assert HEADS * HD == E and EB == 2 * PAIR
    assert EXPERTS == 8 and TOKENS == BANK and NP == 4 and HT == 6

    W1A, W1B = slice(0, HID), slice(HID, 2 * HID)

    QUARTERS = 4

    with ExitStack() as ctx:
        def sb(name, shape, dt=F32):
            return ctx.enter_context(nc.sbuf_tensor(name, shape, dt))

        def sem(name):
            return ctx.enter_context(nc.semaphore(name))

        low = ctx.enter_context(nc.psum_tensor("banks_0_3", [P, 4, BANK], F32))
        high = ctx.enter_context(nc.psum_tensor("banks_4_7", [P, 4, BANK], F32))
        bank = [(low if i < 4 else high)[:, i % 4, :] for i in range(8)]

        ident = sb("ident", [P, P])
        pos_bc = sb("pos_bc", [P, NP, E])
        tokb_bc = sb("tokb_bc", [P, E])
        pos_bias = sb("pos_bias", [P, NP, E])
        w_nat = [sb(f"{n}_nat", [EH, 2, E]) for n in ("wq", "wk", "wv", "wout")]
        wT = [sb(f"{n}T", [EH, 2, E]) for n in ("wq", "wk", "wv")]
        wqk_tail = sb("wqk_tail", [EH, 2, 2, EB])
        woutT_a = sb("woutT_a", [EA, E])
        woutT_b = sb("woutT_b", [P, E])
        BROWS = EXPERTS * HT + 3
        QA, KA, QKB = range(EXPERTS * HT, BROWS)
        bias_rows = sb("bias_rows", [BROWS, P])
        bias_cols = sb("bias_cols", [P, BROWS])
        bout_bc = sb("bout_bc", [P, E])
        bv_bc = sb("bv_bc", [P, E])
        br_bc = sb("br_bc", [P, EXPERTS])
        b2_bc = sb("b2_bc", [P, EXPERTS, E])
        wr_a = sb("wr_a", [EA, EXPERTS])
        wr_b = sb("wr_b", [EB, EXPERTS])
        in_block = sb("in_block", [P, RT, 2])
        in_block2 = sb("in_block2", [P, 2, 2])
        is_head = sb("is_head", [P, 2])
        eps = sb("eps", [P, 1])
        gelu_of_eps = sb("gelu_of_eps", [P, 1])
        expert_no = sb("expert_no", [P, EXPERTS])
        h_tok = sb("h_tok", [P, NP, E])
        h_bout = sb("h_bout", [P, NP, E])
        hT = sb("hT", [EH, 2, TOKENS])
        row_max = [sb(f"row_max{i}", [P, c // IMGS]) for i, c in enumerate(SC)]
        row_sum = [sb(f"row_sum{i}", [P, c // IMGS]) for i, c in enumerate(SC)]
        row_inv = [sb(f"row_inv{i}", [P, c // IMGS]) for i, c in enumerate(SC)]
        attnT_a = sb("attnT_a", [EA, TOKENS])
        attnT_b = sb("attnT_b", [P, TOKENS])
        y1 = sb("y1", [P, NP, E])
        stats = sb("stats", [P, NP, 6])
        mv = sb("mv", [P, NP, 2])
        std = sb("std", [P, NP])
        rstd = sb("rstd", [P, NP])
        x1 = sb("x1", [P, NP, E])
        xa = sb("xa", [P, TOKENS])
        xb = sb("xb", [P, TOKENS])
        xa_hi = sb("xa_hi", [P, TOKENS], F32R)
        xa_lo = sb("xa_lo", [P, TOKENS], F32R)
        xb_hi = sb("xb_hi", [P, TOKENS], F32R)
        xb_lo = sb("xb_lo", [P, TOKENS], F32R)
        logit = sb("logit", [P, NP, EXPERTS])
        lmax = sb("lmax", [P, NP])
        lshift = sb("lshift", [P, NP, EXPERTS])
        lexp = sb("lexp", [P, NP, EXPERTS])
        lsum = sb("lsum", [P, NP])
        linv = sb("linv", [P, NP])
        top = sb("top", [P, NP, 8])
        top_at = sb("top_at", [P, NP, 8], U32)
        top_no = sb("top_no", [P, NP, 8])
        first = sb("first", [P, NP, EXPERTS])
        chosen = sb("chosen", [P, NP, EXPERTS])
        gate_u = sb("gate_u", [P, NP, EXPERTS])
        gate = sb("gate", [P, NP, EXPERTS])
        raw1 = [sb(f"raw1_{i}", [P, 2 * HID]) for i in range(2)]
        raw2 = [sb(f"raw2_{i}", [P, HT, E]) for i in range(2)]
        w1_hi = [sb(f"w1_hi{i}", [P, 2 * HID], F32R) for i in range(2)]
        w1_lo = [sb(f"w1_lo{i}", [P, HID], F32R) for i in range(2)]
        w2_s = [sb(f"w2_s{i}", [P, HT, 2, E], F32R) for i in range(2)]
        acc = sb("acc", [P, NP, 2, E])
        rest = sb("rest", [P, NP, E])
        part = sb("part", [P, NP, E])
        y2 = sb("y2", [P, NP, E])
        y_out = sb("y_out", [P, NP, E])

        def stage(scope):
            return lambda name, shape: scope.enter_context(nc.sbuf_tensor(name, shape, F32))

        with ExitStack() as embedding:
            of = stage(embedding)
            xin = of("xin", [P, PATCH * NP * RUN])
            x_pack = of("x_pack", [P, NP, PATCH_DIM])
            xT = of("xT", [P, KC, TOKENS])
            tokw_sb = of("tokw_sb", [P, KC, E])
        with ExitStack() as attention:
            of = stage(attention)
            q_a = of("q_a", [P, TOKENS])
            q_b = of("q_b", [P, TOKENS])
            k_exp_a = of("k_exp_a", [P, PATCHES, 2, IMGS])
            k_exp_b = of("k_exp_b", [P, PATCHES, 2, IMGS])
            shifted = [of(f"shifted{i}", [P, c]) for i, c in enumerate(SC)]
            expd = [of(f"expd{i}", [P, c]) for i, c in enumerate(SC)]
            prob = [of(f"prob{i}", [P, c]) for i, c in enumerate(SC)]
            probT = [of(f"probT{i}", [P, c]) for i, c in enumerate(SC)]
            attn_first = of("attn_first", [P, TOKENS])
            v_raw = of("v_raw", [P, NP, E])
            v_tok = of("v_tok", [P, NP, E])
        RAW = 3
        h_raw = [sb(f"h_raw{i}", [P, TOKENS]) for i in range(RAW)]
        h_hi = [sb(f"h_hi{i}", [P, HT, TOKENS], F32R) for i in range(2)]
        h_lo = [sb(f"h_lo{i}", [P, HT, TOKENS], F32R) for i in range(2)]

        x_in = [sem(f"x_in{i}") for i in range(QUARTERS)]
        bias_in = sem("bias_in")
        w_in = [sem(f"w_in{i}") for i in range(4)]
        tokw_in = [sem(f"tokw_in{i}") for i in range(2)]
        pos_in = sem("pos_in")
        small_in = sem("small_in")
        raw1_in = [sem(f"raw1_in{i}") for i in range(2)]
        raw2_in = [sem(f"raw2_in{i}") for i in range(2)]
        out_done = sem("out_done")
        pool_step = sem("pool_step")
        ident_ready = sem("ident_ready")
        pos_ready = sem("pos_ready")
        masks_ready = sem("masks_ready")
        tp_full = sem("tp_full")
        tp_act = sem("tp_act")
        tp_dve = sem("tp_dve")
        pack_ready = [sem(f"pack_ready{i}") for i in range(QUARTERS)]
        h_done = sem("h_done")
        h_dve = sem("h_dve")
        hb_ready = sem("hb_ready")
        qk_done = sem("qk_done")
        v_done = sem("v_done")
        q_ready = sem("q_ready")
        k_ready = sem("k_ready")
        v_raw_ready = sem("v_raw_ready")
        v_ready = sem("v_ready")
        score_done = sem("score_done")
        smax = sem("smax")
        ssub = sem("ssub")
        sexp = sem("sexp")
        ssum = sem("ssum")
        sinv = sem("sinv")
        prob_ready = sem("prob_ready")
        probT_ready = sem("probT_ready")
        attn_done = sem("attn_done")
        attn_step = sem("attn_step")
        attnT_ready = sem("attnT_ready")
        attnT_b_ready = sem("attnT_b_ready")
        proj_done = sem("proj_done")
        y1_ready = sem("y1_ready")
        stats_ready = sem("stats_ready")
        mv_ready = sem("mv_ready")
        rstd_ready = sem("rstd_ready")
        ln_std = sem("ln_std")
        x1_ready = sem("x1_ready")
        x1T_done = sem("x1T_done")
        x_copied = sem("x_copied")
        xa_hi_ready = sem("xa_hi_ready")
        xb_hi_ready = sem("xb_hi_ready")
        xlo_ready = sem("xlo_ready")
        logit_done = sem("logit_done")
        lmax_ready = sem("lmax_ready")
        rt = sem("rt")
        rt_exp = sem("rt_exp")
        gate_ready = sem("gate_ready")
        rest_ready = sem("rest_ready")
        part_ready = sem("part_ready")
        w1_hi_ready = sem("w1_hi_ready")
        w1_lo_ready = sem("w1_lo_ready")
        w2_hi_ready = sem("w2_hi_ready")
        w2_lo_ready = sem("w2_lo_ready")
        s1_done = sem("s1_done")
        gelu_done = sem("gelu_done")
        h_lo_ready = sem("h_lo_ready")
        s2_done = sem("s2_done")
        acc_folded = sem("acc_folded")
        folded = sem("folded")
        acc_ready = sem("acc_ready")
        y2_ready = sem("y2_ready")
        out_ready = sem("out_ready")
        last_out_ready = sem("last_out_ready")

        x_src = x.rearrange("b (hp i) w c -> hp b (i w c)", hp=NP)
        x_part = xin.shape[1] // QUARTERS
        x_runs = xin[:, :].rearrange("p (s i wp r) -> p s wp i r", s=QUARTERS, i=PATCH // QUARTERS,
                                      wp=NP)
        x_pack_runs = x_pack[:, :, :].rearrange("p wp (s i r) -> p s wp i r", s=QUARTERS,
                                                  i=PATCH // QUARTERS)
        tokw_src = tok_w.rearrange("(c p) e -> p c e", p=P)
        out_dst = out.rearrange("b (hp wp) e -> wp hp b e", hp=NP)
        w2_src = w2.rearrange("e (t p) d -> e p t d", p=P)

        T_X = [0, 3, 2, 5, 6, 7]
        T_WQ, T_WK, T_BIAS, T_H, T_WV, T_WOUT = 1, 4, 8, 9, 11, 12

        def wait_item_slot(pe, n):
            if n >= 4:
                pe.wait_ge(tp_dve if n % 2 else tp_act, (n - 4) // 2 + 1)

        def tile_bank(t, par):
            return (t + 2 * par) % 4

        ORDER = [("up", 0), ("up", 1), ("down", 0), ("up", 2), ("down", 1), ("up", 3), ("up", 4),
                 ("down", 2), ("up", 5), ("down", 3)]

        LAST_ORDER = [("up", 0), ("up", 1), ("down", 0), ("up", 2), ("down", 1), ("up", 3), ("up", 4),
                      ("up", 5), ("down", 2), ("down", 3)]

        LAST_ORDER_DVE = [("up", 0), ("up", 1), ("up", 2), ("down", 0), ("down", 1), ("up", 3),
                          ("up", 4), ("up", 5), ("down", 2), ("down", 3)]

        def by_patch(a):
            return a.rearrange("p (wp hp q) -> p hp wp q", wp=NP, hp=NP)

        block = ctx.enter_context(nc.Block())

        @block.sync
        def _(sp):
            def load_x(part):
                cols = slice(x_part * part, x_part * (part + 1))
                sp.dma_start(xin[:, cols], x_src[:, :, cols]).then_inc(x_in[part], 16)

            def load_w(n, w):
                sp.dma_start(w_nat[n][:, :, :], w.rearrange("(c p) e -> p c e", p=EH)) \
                    .then_inc(w_in[n], 16)

            def load_tokw(half):
                chunks = slice(KC // 2 * half, KC // 2 * (half + 1))
                sp.dma_start(tokw_sb[:, chunks, :], tokw_src[:, chunks, :]).then_inc(tokw_in[half], 16)

            load_x(0)
            load_tokw(0)
            load_x(1)
            load_w(1, wk)
            load_x(2)
            load_tokw(1)
            load_x(3)
            sp.dma_start(bias_rows[0:EXPERTS * HT, :],
                         b1.rearrange("e (t p) -> (e t) p", p=P)).then_inc(bias_in, 16)
            for row, src in ((QA, bq), (KA, bk)):
                src = src.unsqueeze(0)
                sp.dma_start(bias_rows[row:row + 1, :], src[:, 0:EA]).then_inc(bias_in, 16)
                half = slice(EB * (row - QA), EB * (row - QA + 1))
                sp.dma_start(bias_rows[QKB:QKB + 1, half], src[:, EA:E]).then_inc(bias_in, 16)
            load_w(2, wv)
            load_w(3, wout)

            def load_w1(e, slot):
                sp.dma_start(raw1[slot][:, W1A], w1[e, 0:EA, :]).then_inc(raw1_in[slot], 16)
                for half in range(2):
                    sp.dma_start(raw1[slot][EB * half:EB * (half + 1), W1B], w1[e, EA:E, :]) \
                        .then_inc(raw1_in[slot], 16)

            def load_w2(e, slot):
                sp.dma_start(raw2[slot][:, :, :], w2_src[e]).then_inc(raw2_in[slot], 16)

            for e in range(2):
                load_w1(e, e)
                load_w2(e, e)
            with sp.Fori(0, (EXPERTS - 2) // 2) as i:
                for j in range(2):
                    e = i * 2 + j
                    sp.wait_ge(w1_lo_ready, i * 4 + 2 * (j + 1))
                    load_w1(e + 2, j)
                    sp.wait_ge(w2_lo_ready, i * 2 + (j + 1))
                    load_w2(e + 2, j)
            for wp in range(NP):
                if wp < NP - 1:
                    sp.wait_ge(out_ready, wp + 1)
                else:
                    sp.wait_ge(last_out_ready, 1)
                sp.dma_start(out_dst[wp], y_out[:, wp, :]) \
                    .then_inc(out_done, 16)
            sp.wait_ge(out_done, 16 * NP)

        @block.gpsimd
        def _(pool):
            steps = [0]

            def chain(ins):
                steps[0] += 1
                ins.then_inc(pool_step, 1)
                pool.wait_ge(pool_step, steps[0])

            chain(nc.gpsimd.memset(ident[:, :], 0.0))
            nc.gpsimd.affine_select(out=ident[:, :], in_=ident[:, :], compare_op=ALU.not_equal,
                                    fill=1.0, base=0, pattern=[[-1, P]],
                                    channel_multiplier=1).then_inc(ident_ready, 1)
            chain(nc.gpsimd.memset(in_block[:, :, :], 1.0))
            chain(nc.gpsimd.affine_select(out=in_block[:, :, :], in_=in_block[:, :, :],
                                          compare_op=ALU.is_ge, fill=0.0, base=0,
                                          pattern=[[-PAIR, RT], [-HD, 2]], channel_multiplier=1))
            chain(nc.gpsimd.affine_select(out=in_block[:, :, :], in_=in_block[:, :, :],
                                          compare_op=ALU.is_ge, fill=0.0, base=HD - 1,
                                          pattern=[[PAIR, RT], [HD, 2]], channel_multiplier=-1))
            chain(nc.gpsimd.tensor_tensor(in_block2[:, :, :], in_block[:, 0:2, :],
                                          in_block[:, 2:4, :], ALU.add))
            chain(nc.gpsimd.tensor_tensor(is_head[:, :], in_block2[:, 0, :], in_block2[:, 1, :],
                                          ALU.add))
            chain(nc.gpsimd.iota(expert_no[:, :], pattern=[[1, EXPERTS]], base=0,
                                 channel_multiplier=0, allow_small_or_imprecise_dtypes=True))
            nc.gpsimd.memset(eps[:, :], LN_EPS).then_inc(masks_ready, 1)
            pool.wait_ge(x_in[1], 16)
            pool.dma_start(pos_bc[:, :, :].rearrange("p w e -> p (w e)"),
                           pos.rearrange("(hp w) e -> hp (w e)", w=NP).unsqueeze(1)
                           .broadcast_to([NP, IMGS, NP * E])).then_inc(pos_in, 16)
            pool.dma_start(tokb_bc[:, :], tok_b.partition_broadcast(P)).then_inc(pos_in, 16)
            pool.dma_start(bv_bc[:, :], bv.partition_broadcast(P)).then_inc(small_in, 16)
            pool.dma_start(bout_bc[:, :], bout.partition_broadcast(P)).then_inc(small_in, 16)
            pool.dma_start(br_bc[:, :], br.partition_broadcast(P)).then_inc(small_in, 16)
            pool.dma_start(b2_bc[:, :, :].rearrange("p a e -> p (a e)"),
                           b2.rearrange("a e -> (a e)").partition_broadcast(P)).then_inc(small_in, 16)
            pool.dma_start(wr_a[:, :], wr[0:EA, :]).then_inc(small_in, 16)
            pool.dma_start(wr_b[:, :], wr[EA:E, :]).then_inc(small_in, 16)

            def split_w1(slot, e):
                pool.wait_ge(w1_hi_ready, e + 1)
                nc.gpsimd.tensor_tensor(w1_lo[slot][:, :], raw1[slot][:, W1A],
                                        w1_hi[slot][:, W1A].bitcast(F32), ALU.subtract) \
                    .then_inc(w1_lo_ready, 1)
                pool.wait_ge(w1_lo_ready, e * 2 + 1)
                tail = w1_hi[slot][EB:P, W1B]
                nc.gpsimd.tensor_tensor(tail, raw1[slot][EB:P, W1B], tail.bitcast(F32),
                                        ALU.subtract).then_inc(w1_lo_ready, 1)
                pool.wait_ge(w1_lo_ready, e * 2 + 2)

            def split_w2(slot, e):
                pool.wait_ge(w2_hi_ready, e + 1)
                nc.gpsimd.tensor_tensor(w2_s[slot][:, :, 1, :], raw2[slot][:, :, :],
                                        w2_s[slot][:, :, 0, :].bitcast(F32), ALU.subtract) \
                    .then_inc(w2_lo_ready, 1)

            pool.wait_ge(pos_in, 16 * 2)
            nc.gpsimd.tensor_tensor(pos_bias[:, :, :], pos_bc[:, :, :],
                                    tokb_bc[:, :].unsqueeze(1).broadcast_to([P, NP, E]),
                                    ALU.add).then_inc(pos_ready, 1)
            pool.wait_ge(small_in, 16 * 6)
            pool.wait_ge(h_dve, NP)
            nc.gpsimd.tensor_tensor(h_bout[:, :, :], h_tok[:, :, :],
                                    bout_bc[:, :].unsqueeze(1).broadcast_to([P, NP, E]),
                                    ALU.add).then_inc(hb_ready, 1)
            split_w1(0, 0)
            def normalise(r):
                pool.wait_ge(sinv, r + 1)
                nc.gpsimd.tensor_tensor(
                    prob[r][:, :].rearrange("p (a k) -> p a k", k=IMGS),
                    expd[r][:, :].rearrange("p (a k) -> p a k", k=IMGS),
                    row_inv[r][:, :].unsqueeze(2).broadcast_to([P, SC[r] // IMGS, IMGS]),
                    ALU.mult).then_inc(prob_ready, 1)

            normalise(0)
            normalise(1)
            pool.wait_ge(v_raw_ready, 2)
            nc.gpsimd.tensor_tensor(v_tok[:, :, :], v_raw[:, :, :],
                                    bv_bc[:, :].unsqueeze(1).broadcast_to([P, NP, E]),
                                    ALU.add).then_inc(v_ready, 1)
            normalise(2)
            normalise(3)
            split_w1(1, 1)
            split_w2(0, 0)
            with pool.Fori(0, (EXPERTS - 2) // 2) as i:
                for j in range(2):
                    split_w1(j, i * 2 + (j + 2))
                    split_w2(1 - j, i * 2 + (j + 1))
            split_w2(1, EXPERTS - 1)
            pool.wait_ge(acc_ready, (EXPERTS - 1) * NP)
            nc.gpsimd.tensor_tensor(acc[:, :, 0, :], acc[:, :, 0, :], acc[:, :, 1, :],
                                    ALU.add).then_inc(acc_folded, 1)
            pool.wait_ge(acc_folded, 1)
            pool.wait_ge(rest_ready, (EXPERTS + 1) * NP)
            nc.gpsimd.tensor_tensor(rest[:, :, :], rest[:, :, :], acc[:, :, 0, :],
                                    ALU.add).then_inc(folded, 1)
            for wp in range(NP - 1):
                pool.wait_ge(rstd_ready, NP + wp + 1)
                nc.gpsimd.tensor_scalar(y_out[:, wp, :], y2[:, wp, :], mv[:, wp, 0:1],
                                        rstd[:, wp:wp + 1], ALU.subtract, ALU.mult) \
                    .then_inc(out_ready, 1)

        @block.scalar
        def _(act):
            act.dma_start(w_nat[0][:, :, :], wq.rearrange("(c p) e -> p c e", p=EH)) \
                .then_inc(w_in[0], 16)

            def take_item(n, dst, src):
                act.wait_ge(tp_full, n + 1)
                nc.scalar.copy(dst, src).then_inc(tp_act, 1)

            def pack(part):
                act.wait_ge(x_in[part], 16)
                nc.scalar.copy(x_pack_runs[:, part, 3], x_runs[:, part, 3]).then_inc(pack_ready[part], 1)

            pack(0)
            take_item(0, xT[:, 0, :], bank[0])
            pack(1)
            pack(2)
            take_item(2, xT[:, 2, :], bank[2])
            pack(3)
            act.wait_ge(tp_full, T_WK + 1)
            nc.scalar.copy(wqk_tail[:, :, 1, :], bank[0][0:EH, 0:2 * E]
                           .rearrange("p (c e) -> p c e", c=2)[:, :, EA:E])
            take_item(T_WK, wT[1][:, :, :].rearrange("p c e -> p (c e)"), bank[0][0:EH, 0:2 * E])
            take_item(6, xT[:, 4, :], bank[2])
            take_item(T_BIAS, bias_cols[:, :], bank[0][:, 0:BROWS])
            take_item(T_H + 1, hT[:, 1, :], bank[(T_H + 1) % 4][0:EH, :])
            act.wait_ge(tp_full, T_WOUT + 1)
            nc.scalar.copy(woutT_b[:, :], bank[T_WOUT % 4][:, E:2 * E])
            take_item(T_WOUT, woutT_a[:, :], bank[T_WOUT % 4][:, 0:E])
            act.wait_ge(qk_done, 2)
            nc.scalar.activation(q_a[:, :], bank[0], ACT.Identity,
                                 bias=bias_cols[:, QA:QA + 1]).then_inc(q_ready, 1)
            act.wait_ge(qk_done, 3)
            act.wait_ge(k_ready, 2)
            nc.scalar.activation(q_b[EB:P, :], bank[6][0:EB, :], ACT.Identity,
                                 bias=bias_cols[0:EB, QKB:QKB + 1]).then_inc(q_ready, 1)
            def copy_v(w):
                act.wait_ge(v_done, w + 1)
                nc.scalar.copy(v_raw[:, 2 * w:2 * w + 2, :].rearrange("p a e -> p (a e)"),
                               bank[4 + w][:, 0:2 * E]).then_inc(v_raw_ready, 1)

            def exponentials(r):
                act.wait_ge(ssub, r + 1)
                nc.scalar.activation(expd[r][:, :], shifted[r][:, :], ACT.Exp,
                                     scale=SCALE).then_inc(sexp, 1)

            exponentials(0)
            copy_v(0)
            exponentials(1)
            copy_v(1)
            exponentials(2)
            exponentials(3)
            act.wait_ge(attn_done, 1)
            tail = low[EB:P, :, 0:AS].rearrange("p hp (wp h q) -> p hp wp h q", h=2, q=IMGS)
            for h in range(2):
                nc.scalar.activation(by_patch(attnT_b[EB * h:EB * (h + 1), :]), tail[:, :, :, h, :],
                                     ACT.Copy, scale=is_head[EB:P, h:h + 1]) \
                    .then_inc(attnT_b_ready, 1)
            for wp in range(NP):
                act.wait_ge(mv_ready, wp + 1)
                nc.scalar.activation(std[:, wp:wp + 1], mv[:, wp, 1:2], ACT.Sqrt,
                                     bias=eps[:, 0:1]).then_inc(ln_std, 1)
            nc.scalar.activation(gelu_of_eps[:, :], eps[:, :], ACT.Gelu)
            act.wait_ge(x1T_done, 1)
            nc.scalar.copy(xa_hi[:, :], bank[4]).then_inc(xa_hi_ready, 1)
            act.wait_ge(xb_hi_ready, 1)
            nc.scalar.copy(xb[:, :], bank[5]).then_inc(x_copied, 1)
            act.wait_ge(xlo_ready, 1)
            nc.scalar.copy(xa[:, :], bank[4]).then_inc(x_copied, 1)

            def gelu(tile, n, b1_col, par, h_free):
                act.wait_ge(s1_done, n + 1)
                bias = bias_cols[:, bass.ds(b1_col, 1)]
                src = bank[tile_bank(tile, par)][:, :]
                if h_free is not None:
                    h_free()
                nc.scalar.activation(h_raw[tile % RAW][:, :], src, ACT.Gelu, bias=bias) \
                    .then_inc(gelu_done, 1)
                nc.scalar.activation(h_hi[par][:, tile, :], src, ACT.Gelu, bias=bias) \
                    .then_inc(gelu_done, 1)

            for t in range(HT):
                def free(t=t):
                    if t >= RAW:
                        act.wait_ge(h_lo_ready, t - RAW + 1)
                gelu(t, t, t, 0, free)
            act.wait_ge(rt, 2)
            nc.scalar.activation(lexp[:, :, :], lshift[:, :, :], ACT.Exp).then_inc(rt_exp, 1)

            def up_step(e, par_next):
                for t in range(HT):
                    n = e * HT + (HT + t)

                    def free(t=t, n=n):
                        act.wait_ge(h_lo_ready, n - (RAW - 1))
                        if t == 0:
                            act.wait_ge(acc_ready, e * NP + NP)
                    gelu(t, n, n, par_next, free)

            with act.Fori(0, (EXPERTS - 2) // 2) as i:
                for j in range(2):
                    up_step(i * 2 + j, 1 - j)
            up_step(EXPERTS - 2, 1)
            for wp in range(NP):
                act.wait_ge(mv_ready, NP + wp + 1)
                nc.scalar.activation(std[:, wp:wp + 1], mv[:, wp, 1:2], ACT.Sqrt,
                                     bias=eps[:, 0:1]).then_inc(ln_std, 1)

        @block.vector
        def _(dve):
            def take_item(n, dst, src):
                dve.wait_ge(tp_full, n + 1)
                nc.vector.tensor_copy(dst, src).then_inc(tp_dve, 1)

            nc.vector.memset(acc[:, :, :, :], 0.0).then_inc(acc_ready, NP)
            dve.wait_ge(ident_ready, 1)

            def hi_w1(slot, landed):
                dve.wait_ge(raw1_in[slot], landed)
                nc.vector.tensor_copy(w1_hi[slot][:, :], raw1[slot][:, :]).then_inc(w1_hi_ready, 1)

            def hi_w2(slot, landed):
                dve.wait_ge(raw2_in[slot], landed)
                nc.vector.tensor_copy(w2_s[slot][:, :, 0, :], raw2[slot][:, :, :]) \
                    .then_inc(w2_hi_ready, 1)

            def pack(part):
                dve.wait_ge(x_in[part], 16)
                for wp in range(3):
                    nc.vector.tensor_copy(x_pack_runs[:, part, wp], x_runs[:, part, wp]) \
                        .then_inc(pack_ready[part], 1)

            pack(0)
            pack(1)
            dve.wait_ge(tp_full, T_WQ + 1)
            nc.vector.tensor_copy(wqk_tail[:, :, 0, :], bank[1][0:EH, 0:2 * E]
                                  .rearrange("p (c e) -> p c e", c=2)[:, :, EA:E])
            take_item(T_WQ, wT[0][:, :, :].rearrange("p c e -> p (c e)"), bank[1][0:EH, 0:2 * E])
            pack(2)
            take_item(3, xT[:, 1, :], bank[3])
            pack(3)
            take_item(5, xT[:, 3, :], bank[1])
            take_item(7, xT[:, 5, :], bank[3])
            dve.wait_ge(pos_ready, 1)
            for wp in range(NP):
                dve.wait_ge(h_done, wp + 1)
                nc.vector.tensor_tensor(h_tok[:, wp, :], bank[4 + wp][:, 0:E], pos_bias[:, wp, :],
                                        ALU.add).then_inc(h_dve, 1)
            take_item(T_H, hT[:, 0, :], bank[T_H % 4][0:EH, :])
            take_item(T_WV, wT[2][:, :, :].rearrange("p c e -> p (c e)"),
                      bank[T_WV % 4][0:EH, 0:2 * E])
            hi_w1(0, 48)

            dve.wait_ge(masks_ready, 1)
            dve.wait_ge(tp_act, T_BIAS // 2 + 1)

            def expand_k(dst, src, rows, col):
                for h in range(2):
                    ins = nc.vector.tensor_scalar(dst[rows, :, h, :],
                                                  src.rearrange("p (a k) -> p a k", k=IMGS),
                                                  bias_cols[rows, col:col + 1],
                                                  is_head[rows, h:h + 1], ALU.add, ALU.mult)
                ins.then_inc(k_ready, 1)

            dve.wait_ge(qk_done, 1)
            expand_k(k_exp_a, bank[1], slice(0, P), KA)
            dve.wait_ge(qk_done, 3)
            expand_k(k_exp_b, bank[6][EB:P, :], slice(EB, P), QKB)

            def shift(r):
                scores = bank[r][:, 0:SC[r]].rearrange("p (a k) -> p a k", k=IMGS)
                dve.wait_ge(score_done, r + 1)
                nc.vector.tensor_reduce(row_max[r][:, :], scores, AX, ALU.max).then_inc(smax, 1)
                dve.wait_ge(smax, r + 1)
                nc.vector.tensor_tensor(
                    shifted[r][:, :].rearrange("p (a k) -> p a k", k=IMGS), scores,
                    row_max[r][:, :].unsqueeze(2).broadcast_to([P, SC[r] // IMGS, IMGS]),
                    ALU.subtract).then_inc(ssub, 1)

            def invert(r):
                dve.wait_ge(sexp, r + 1)
                nc.vector.tensor_reduce(row_sum[r][:, :],
                                        expd[r][:, :].rearrange("p (a k) -> p a k", k=IMGS),
                                        AX, ALU.add).then_inc(ssum, 1)
                dve.wait_ge(ssum, r + 1)
                nc.vector.reciprocal(row_inv[r][:, :], row_sum[r][:, :]).then_inc(sinv, 1)

            def turn(r):
                dve.wait_ge(prob_ready, r + 1)
                nc.vector.transpose(probT[r][:, :], prob[r][:, :]).then_inc(probT_ready, 1)

            shift(0)
            shift(1)
            invert(0)
            invert(1)
            turn(0)
            shift(2)
            turn(1)
            shift(3)
            invert(2)
            invert(3)
            turn(2)
            turn(3)
            hi_w2(0, 16)
            hi_w1(1, 48)
            both = high[:, :, 0:AS].rearrange("p hp (wp h q) -> p hp wp h q", h=2, q=IMGS)
            dve.wait_ge(attn_done, 2)

            def first_head(wp):
                nc.vector.tensor_scalar(by_patch(attn_first[:, :])[:, :, wp, :],
                                        both[:, :, wp, 0, :], is_head[:, 0:1], None,
                                        ALU.mult).then_inc(attn_step, 1)

            def second_head(wp):
                dve.wait_ge(attn_step, wp + 1)
                nc.vector.scalar_tensor_tensor(
                    out=by_patch(attnT_a[:, :])[:, :, wp, :], in0=both[:, :, wp, 1, :],
                    scalar=is_head[:, 1:2], in1=by_patch(attn_first[:, :])[:, :, wp, :],
                    op0=ALU.mult, op1=ALU.add).then_inc(attnT_ready, 1)

            first_head(0)
            second_head(0)
            for wp in range(1, NP):
                first_head(wp)
                if wp > 1:
                    second_head(wp - 1)
            second_head(NP - 1)

            def add1(wp):
                dve.wait_ge(proj_done, wp + 1)
                nc.vector.tensor_tensor(y1[:, wp, :], bank[wp][:, 0:E], h_bout[:, wp, :],
                                        ALU.add).then_inc(y1_ready, 1)

            def bn_stats(y, y_sem, wp, norm):
                dve.wait_ge(y_sem, wp + 1)
                nc.vector.bn_stats(stats[:, wp, :], y[:, wp, :]).then_inc(stats_ready, 1)

            def bn_aggr(wp, norm):
                dve.wait_ge(stats_ready, NP * norm + wp + 1)
                nc.vector.bn_aggr(mv[:, wp, :], stats[:, wp, :]).then_inc(mv_ready, 1)

            def invert_std(wp, norm):
                dve.wait_ge(ln_std, NP * norm + wp + 1)
                nc.vector.reciprocal(rstd[:, wp:wp + 1], std[:, wp:wp + 1]).then_inc(rstd_ready, 1)

            def scale(dst, y, wp, norm, ready):
                dve.wait_ge(rstd_ready, NP * norm + wp + 1)
                nc.vector.tensor_scalar(dst[:, wp, :], y[:, wp, :], mv[:, wp, 0:1],
                                        rstd[:, wp:wp + 1], ALU.subtract, ALU.mult).then_inc(ready, 1)

            dve.wait_ge(hb_ready, 1)
            add1(0)
            for wp in range(NP):
                bn_stats(y1, y1_ready, wp, 0)
                if wp:
                    invert_std(wp - 1, 0)
                if wp < NP - 1:
                    add1(wp + 1)
                if wp:
                    scale(x1, y1, wp - 1, 0, x1_ready)
                bn_aggr(wp, 0)
            invert_std(NP - 1, 0)
            scale(x1, y1, NP - 1, 0, x1_ready)
            dve.wait_ge(x1T_done, 1)
            nc.vector.tensor_copy(xb_hi[:, :], bank[5]).then_inc(xb_hi_ready, 1)
            dve.wait_ge(xa_hi_ready, 1)
            nc.vector.tensor_tensor(xa_lo[:, :], bank[4], xa_hi[:, :].bitcast(F32),
                                    ALU.subtract).then_inc(xlo_ready, 1)
            dve.wait_ge(xb_hi_ready, 1)
            dve.wait_ge(x_copied, 1)
            nc.vector.tensor_tensor(xb_lo[:, :], bank[5], xb_hi[:, :].bitcast(F32),
                                    ALU.subtract).then_inc(xlo_ready, 1)

            rt_count = [0]

            def rt_step(ins, wait=True):
                rt_count[0] += 1
                ins.then_inc(rt, 1)
                if wait:
                    dve.wait_ge(rt, rt_count[0])

            def by_tile(a):
                return a.unsqueeze(2).broadcast_to([P, NP, EXPERTS])

            def h_split(t, par, gelus):
                dve.wait_ge(gelu_done, gelus)
                nc.vector.tensor_tensor(h_lo[par][:, t, :], h_raw[t % RAW][:, :],
                                        h_hi[par][:, t, :].bitcast(F32), ALU.subtract) \
                    .then_inc(h_lo_ready, 1)

            for t in range(3):
                h_split(t, 0, 2 * (t + 1))
            dve.wait_ge(logit_done, 1)
            rt_step(nc.vector.tensor_tensor(
                logit[:, :, :], bank[6][:, 0:NP * EXPERTS].rearrange("p (a e) -> p a e", a=NP),
                br_bc[:, :].unsqueeze(1).broadcast_to([P, NP, EXPERTS]), ALU.add))
            nc.vector.tensor_reduce(lmax[:, :], logit[:, :, :], AX, ALU.max).then_inc(lmax_ready, 1)
            dve.wait_ge(lmax_ready, 1)
            rt_step(nc.vector.tensor_tensor(lshift[:, :, :], logit[:, :, :], by_tile(lmax[:, :]),
                                            ALU.subtract), wait=False)

            for t in range(3, HT):
                h_split(t, 0, 2 * (t + 1))
            nc.vector.tensor_copy(rest[:, :, :], x1[:, :, :]).then_inc(rest_ready, NP)
            dve.wait_ge(rt_exp, 1)
            nc.vector.tensor_reduce(lsum[:, :], lexp[:, :, :], AX, ALU.add).then_inc(rt, 1)
            for wp in range(NP):
                nc.vector.max(top[:, wp, :], lexp[:, wp, :]).then_inc(rt, 1)
            rt_count[0] += 1 + NP
            dve.wait_ge(rt, rt_count[0])
            nc.vector.reciprocal(linv[:, :], lsum[:, :]).then_inc(rt, 1)
            for wp in range(NP):
                nc.vector.max_index(top_at[:, wp, :], top[:, wp, :], lexp[:, wp, :]).then_inc(rt, 1)
            rt_count[0] += 1 + NP
            dve.wait_ge(rt, rt_count[0])
            rt_step(nc.vector.tensor_copy(top_no[:, :, :], top_at[:, :, :]))
            for wp in range(NP):
                rt_step(nc.vector.tensor_scalar(first[:, wp, :], expert_no[:, :],
                                                top_no[:, wp, 0:1], None, ALU.is_equal), wait=False)
            dve.wait_ge(rt, rt_count[0])
            for wp in range(NP):
                rt_step(nc.vector.scalar_tensor_tensor(
                    out=chosen[:, wp, :], in0=expert_no[:, :], scalar=top_no[:, wp, 1:2],
                    in1=first[:, wp, :], op0=ALU.is_equal, op1=ALU.add), wait=False)
            dve.wait_ge(rt, rt_count[0])
            rt_step(nc.vector.tensor_tensor(gate_u[:, :, :], lexp[:, :, :], chosen[:, :, :],
                                            ALU.mult))
            nc.vector.tensor_tensor(gate[:, :, :], gate_u[:, :, :], by_tile(linv[:, :]),
                                    ALU.mult).then_inc(gate_ready, 1)
            dve.wait_ge(gate_ready, 1)

            def add_b2(e, wp):
                dve.wait_ge(rest_ready, e * NP + (wp + 1))
                nc.vector.scalar_tensor_tensor(
                    out=rest[:, wp, :], in0=b2_bc[:, bass.ds(e, 1), :].rearrange("p a e -> p (a e)"),
                    scalar=gate[:, wp, bass.ds(e, 1)], in1=rest[:, wp, :],
                    op0=ALU.mult, op1=ALU.add).then_inc(rest_ready, 1)

            def combine(e, wp):
                dve.wait_ge(s2_done, e * NP + (wp + 1))
                dve.wait_ge(acc_ready, e * NP + (wp + 1))
                nc.vector.scalar_tensor_tensor(
                    out=acc[:, wp, :, :].rearrange("p a e -> p (a e)"), in0=bank[4 + wp][:, 0:2 * E],
                    scalar=gate[:, wp, bass.ds(e, 1)],
                    in1=acc[:, wp, :, :].rearrange("p a e -> p (a e)"),
                    op0=ALU.mult, op1=ALU.add).then_inc(acc_ready, 1)

            def add_output(e, wp, dst, dst_sem):
                dve.wait_ge(s2_done, e * NP + wp + 1)
                if e < EXPERTS - 1:
                    dve.wait_ge(folded, 1)
                nc.vector.scalar_tensor_tensor(
                    out=part[:, wp, :], in0=bank[4 + wp][:, 0:E], scalar=gate[:, wp, e:e + 1],
                    in1=rest[:, wp, :], op0=ALU.mult, op1=ALU.add).then_inc(part_ready, 1)
                if e == EXPERTS - 1 and wp:
                    invert_std(wp - 1, 1)
                dve.wait_ge(part_ready, (e - (EXPERTS - 2)) * NP + wp + 1)
                nc.vector.scalar_tensor_tensor(
                    out=dst[:, wp, :], in0=bank[4 + wp][:, E:2 * E], scalar=gate[:, wp, e:e + 1],
                    in1=part[:, wp, :], op0=ALU.mult, op1=ALU.add).then_inc(dst_sem, 1)

            def step(e, par, landed1, landed2, last=False):
                if landed1 is not None:
                    hi_w1(par, landed1)
                hi_w2(1 - par, landed2)
                for kind, k in LAST_ORDER_DVE if last else ORDER:
                    if kind == "up":
                        h_split(k, 1 - par, (e * HT + (HT + k + 1)) * 2)
                        if last and k < 2:
                            for wp in range(NP):
                                add_b2(EXPERTS - 2 + k, wp)
                    elif last:
                        add_output(e, k, rest, acc_ready)
                    else:
                        combine(e, k)
                        add_b2(e, k)

            with dve.Fori(0, (EXPERTS - 2) // 2) as i:
                step(i * 2, 0, (i + 2) * 48, (i + 1) * 16)
                step(i * 2 + 1, 1, (i + 2) * 48, (i + 2) * 16)
            step(EXPERTS - 2, 0, None, 16 * (EXPERTS // 2), last=True)
            last = EXPERTS - 1

            for wp in range(NP):
                dve.wait_ge(acc_ready, last * NP + wp + 1)
                add_output(last, wp, y2, y2_ready)
                bn_stats(y2, y2_ready, wp, 1)
                bn_aggr(wp, 1)
            invert_std(NP - 1, 1)
            scale(y_out, y2, NP - 1, 1, last_out_ready)

        @block.tensor
        def _(pe):
            def item(n, outs_ins):
                wait_item_slot(pe, n)
                for o, i_ in outs_ins:
                    k = i_.shape[0]
                    mm = pe.transpose(o, i_, ident[0:k, 0:k])
                mm.then_inc(tp_full, 1)

            pe.wait_ge(ident_ready, 1)

            def warm(n, b=bank[7]):
                for _ in range(n):
                    pe.matmul(b[:, BANK - P:BANK], ident[:, 0:b.shape[0]], ident[:, :],
                              start=True, stop=True)

            warm(WARM_START)

            def turn_w(n, w):
                pe.wait_ge(w_in[w], 16)
                item(n, [(bank[n % 4][0:EH, E * ci + EH * co:E * ci + EH * (co + 1)],
                          w_nat[w][:, co, EH * ci:EH * (ci + 1)]) for ci in range(2) for co in range(2)])

            def turn_x(c):
                item(T_X[c], [(bank[T_X[c] % 4][:, P * wp:P * (wp + 1)],
                               x_pack[:, wp, P * c:P * (c + 1)]) for wp in range(NP)])

            def embed(c):
                n = T_X[c]
                pe.wait_ge(tp_dve if n % 2 else tp_act, n // 2 + 1)
                for wp in range(NP):
                    mm = pe.matmul(bank[4 + wp][:, 0:E], xT[:, c, P * wp:P * (wp + 1)],
                                   tokw_sb[:, c, :], start=(c == 0), stop=(c == KC - 1))
                    if c == KC - 1:
                        mm.then_inc(h_done, 1)

            pe.wait_ge(pack_ready[0], NP)
            turn_x(0)
            turn_w(T_WQ, 0)
            pe.wait_ge(tokw_in[0], 16)
            embed(0)
            pe.wait_ge(pack_ready[1], NP)
            turn_x(2)
            turn_x(1)
            turn_w(T_WK, 1)
            embed(2)
            embed(1)
            pe.wait_ge(pack_ready[2], NP)
            turn_x(3)
            pe.wait_ge(pack_ready[3], NP)
            turn_x(4)
            turn_x(5)
            pe.wait_ge(tokw_in[1], 16)
            embed(3)
            pe.wait_ge(bias_in, 16 * 5)
            item(T_BIAS, [(bank[T_BIAS % 4][:, 0:BROWS], bias_rows[:, :])])
            embed(4)
            embed(5)
            pe.wait_ge(h_dve, NP)
            for ci in range(2):
                n = T_H + ci
                item(n, [(bank[n % 4][0:EH, P * wp:P * (wp + 1)],
                          h_tok[:, wp, EH * ci:EH * (ci + 1)]) for wp in range(NP)])
            turn_w(T_WV, 2)
            pe.wait_ge(w_in[3], 16)
            wait_item_slot(pe, T_WOUT)
            for half in range(2):
                for co in range(2):
                    pe.matmul(bank[T_WOUT % 4][EB * half:EB * (half + 1),
                                               E + EH * co:E + EH * (co + 1)],
                              w_nat[3][:, co, EA:E], ident[0:EH, 0:EH], start=True, stop=True)
            item(T_WOUT, [(bank[T_WOUT % 4][:, EH * co:EH * (co + 1)], w_nat[3][:, co, 0:EA])
                          for co in range(2)])
            pe.wait_ge(tp_dve, T_H // 2 + 1)
            pe.wait_ge(tp_act, (T_H + 1) // 2 + 1)
            for w in (1, 0):
                if w == 0:
                    pe.wait_ge(tp_act, T_WOUT // 2 + 1)
                for ci in range(2):
                    mm = pe.matmul(bank[w], wT[w][:, ci, 0:EA], hT[:, ci, :],
                                   start=(ci == 0), stop=(ci == 1))
                mm.then_inc(qk_done, 1)
            for ci in range(2):
                mm = pe.matmul(bank[6], wqk_tail[:, ci, :, :].rearrange("p a e -> p (a e)"),
                               hT[:, ci, :], start=(ci == 0), stop=(ci == 1))
            mm.then_inc(qk_done, 1)

            def scores(r):
                rows = slice(PAIR * r, PAIR * (r + 1))
                for q, k_exp, at in ((q_a, k_exp_a, 0), (q_b, k_exp_b, AS))[0:SC[r] // AS]:
                    for a in range(PATCHES):
                        wp, hp = divmod(a, NP)
                        cols = slice(at + 2 * IMGS * wp, at + 2 * IMGS * (wp + 1))
                        mm = pe.matmul(bank[r][IMGS * hp:IMGS * (hp + 1), cols],
                                       q[rows, IMGS * a:IMGS * (a + 1)],
                                       k_exp[rows, a, :, :].rearrange("p h k -> p (h k)"),
                                       start=True, stop=True)
                mm.then_inc(score_done, 1)

            pe.wait_ge(q_ready, 1)
            pe.wait_ge(k_ready, 1)
            scores(0)
            scores(1)
            pe.wait_ge(tp_dve, T_WV // 2 + 1)
            for wp in range(NP):
                for ci in range(2):
                    mm = pe.matmul(bank[4 + wp // 2][:, E * (wp % 2):E * (wp % 2 + 1)],
                                   hT[:, ci, P * wp:P * (wp + 1)],
                                   wT[2][:, ci, :], start=(ci == 0), stop=(ci == 1))
                if wp % 2:
                    mm.then_inc(v_done, 1)
            pe.wait_ge(q_ready, 2)
            pe.wait_ge(k_ready, 2)
            scores(2)
            scores(3)
            pe.wait_ge(v_ready, 1)

            def attend(r):
                pe.wait_ge(probT_ready, r + 1)
                for wp in range(NP):
                    cols = slice(2 * IMGS * wp, 2 * IMGS * (wp + 1))
                    for hp in range(NP):
                        rows = slice(IMGS * hp, IMGS * (hp + 1))
                        mm = pe.matmul(bank[4 + hp][PAIR * r:PAIR * (r + 1), cols],
                                       v_tok[rows, wp, PAIR * r:PAIR * (r + 1)],
                                       probT[r][rows, cols], start=True, stop=True)
                return mm

            def attend_tail(r):
                pair = r - 2
                for wp in range(NP):
                    cols = slice(2 * IMGS * wp, 2 * IMGS * (wp + 1))
                    at = AS + 2 * IMGS * wp
                    for hp in range(NP):
                        rows = slice(IMGS * hp, IMGS * (hp + 1))
                        mm = pe.matmul(bank[hp][PAIR * r:PAIR * (r + 1), cols],
                                       v_tok[rows, wp, EA + PAIR * pair:EA + PAIR * (pair + 1)],
                                       probT[r][rows, at:at + 2 * IMGS], start=True, stop=True)
                return mm

            attend(0)
            attend(1)
            attend(2)
            pe.wait_ge(ssub, RT)
            attend_tail(2)
            pe.wait_ge(probT_ready, RT)
            attend_tail(3).then_inc(attn_done, 1)
            attend(3).then_inc(attn_done, 1)
            warm(WARM_EXTRACT, bank[0][0:EB, :])
            for wp in range(NP):
                tok = slice(P * wp, P * (wp + 1))
                pe.wait_ge(attnT_ready, wp + 1)
                pe.wait_ge(attnT_b_ready, 2)
                pe.matmul(bank[wp][:, 0:E], attnT_b[:, tok], woutT_b[:, :], start=True, stop=False)
                pe.matmul(bank[wp][:, 0:E], attnT_a[:, tok], woutT_a[:, :], start=False, stop=True) \
                    .then_inc(proj_done, 1)
            warm(WARM_NORM)
            for wp in range(NP):
                cols = slice(P * wp, P * (wp + 1))
                pe.wait_ge(x1_ready, wp + 1)
                for half in range(2):
                    pe.matmul(bank[5][EB * half:EB * (half + 1), cols], x1[:, wp, EA:E],
                              ident[:, :], start=True, stop=True)
                head = pe.transpose(bank[4][:, cols], x1[:, wp, 0:EA], ident[:, :])
            head.then_inc(x1T_done, 1)
            warm(WARM_COPY)

            def router_logits():
                pe.wait_ge(x_copied, 2)
                for wp in range(NP):
                    tok = slice(P * wp, P * (wp + 1))
                    dst = bank[6][:, EXPERTS * wp:EXPERTS * (wp + 1)]
                    pe.matmul(dst, xa[:, tok], wr_a[:, :], start=True, stop=False)
                    mm = pe.matmul(dst, xb[0:EB, tok], wr_b[:, :], start=False, stop=True)
                mm.then_inc(logit_done, 1)

            def up_hi(t, par):
                b = bank[tile_bank(t, par)]
                cols = slice(P * t, P * (t + 1))
                tail = slice(HID + P * t, HID + P * (t + 1))
                pe.matmul(b, w1_hi[par][:, cols], xa_hi[:, :], start=True, stop=False)
                pe.matmul(b, w1_lo[par][:, cols], xa_hi[:, :], start=False, stop=False)
                pe.matmul(b, w1_hi[par][:, tail], xb_hi[:, :], start=False, stop=False)

            def up_lo(t, par):
                b = bank[tile_bank(t, par)]
                cols = slice(P * t, P * (t + 1))
                tail = slice(HID + P * t, HID + P * (t + 1))
                pe.matmul(b, w1_hi[par][:, cols], xa_lo[:, :], start=False, stop=False)
                pe.matmul(b, w1_hi[par][:, tail], xb_lo[:, :], start=False, stop=True) \
                    .then_inc(s1_done, 1)

            def up(t, par):
                up_hi(t, par)
                up_lo(t, par)

            def down(wp, par):
                tok = slice(P * wp, P * (wp + 1))

                def hi(t, start=False, stop=False):
                    return pe.matmul(bank[4 + wp][:, 0:2 * E], h_hi[par][:, t, tok],
                                     w2_s[par][:, t, :, :].rearrange("p a e -> p (a e)"),
                                     start=start, stop=stop, skip_group_check=True)

                hi(0, start=True)
                for t in range(HT):
                    pe.matmul(bank[4 + wp][:, 0:E], h_lo[par][:, t, tok], w2_s[par][:, t, 0, :],
                              start=False, stop=False, skip_group_check=True)
                    if t > 0:
                        mm = hi(t, stop=(t == HT - 1))
                mm.then_inc(s2_done, 1)

            pe.wait_ge(xa_hi_ready, 1)
            pe.wait_ge(xb_hi_ready, 1)
            pe.wait_ge(w1_lo_ready, 2)
            up_hi(0, 0)
            up_hi(1, 0)
            pe.wait_ge(xlo_ready, 2)
            up_lo(0, 0)
            up_lo(1, 0)
            for t in range(2, HT):
                if t >= 4:
                    pe.wait_ge(gelu_done, 2 * (t - 4 + 1))
                up(t, 0)
                if t == 3:
                    router_logits()

            def step(e, par, order=ORDER):
                for kind, k in order:
                    if kind == "up":
                        if k == 0:
                            pe.wait_ge(w1_lo_ready, e * 2 + 4)
                        pe.wait_ge(gelu_done, (e * HT + (HT + k - 3)) * 2)
                        up(k, 1 - par)
                    else:
                        if k == 0:
                            pe.wait_ge(w2_lo_ready, e + 1)
                            pe.wait_ge(h_lo_ready, e * HT + HT)
                        pe.wait_ge(acc_ready, e * NP + (k + 1))
                        down(k, par)

            with pe.Fori(0, (EXPERTS - 2) // 2) as i:
                step(i * 2, 0)
                step(i * 2 + 1, 1)
            step(EXPERTS - 2, 0, LAST_ORDER)
            pe.wait_ge(w2_lo_ready, EXPERTS)
            pe.wait_ge(h_lo_ready, EXPERTS * HT)
            for wp in range(NP):
                pe.wait_ge(acc_ready, (EXPERTS - 1) * NP + wp + 1)
                down(wp, 1)


_INS = ["x", "L0_tok_W", "L0_tok_b", "L0_tok_pos_emb", "L0_attn_Wq", "L0_attn_bq", "L0_attn_Wk",
        "L0_attn_bk", "L0_attn_Wv", "L0_attn_bv", "L0_attn_Wout", "L0_attn_bout", "L0_ffn_W1",
        "L0_ffn_b1", "L0_ffn_W2", "L0_ffn_b2", "L0_ffn_Wr", "L0_ffn_br"]


def kernel(**inputs):
    import numpy as np
    import concourse.bacc as bacc
    from concourse.bass_utils import run_bass_kernel_spmd

    nc = bacc.Bacc("TRN2", target_bir_lowering=False, num_devices=1)
    arrays, args = {}, []
    for name in _INS:
        a = np.ascontiguousarray(inputs[name])
        arrays[f"in_{name}_dram"] = a
        args.append(nc.dram_tensor(f"in_{name}_dram", a.shape, mybir.dt.from_np(a.dtype),
                                   kind="ExternalInput").ap())
    images, side = inputs["x"].shape[0], inputs["x"].shape[1]
    shape = (images, (side // PATCH) ** 2, inputs["L0_tok_W"].shape[1])
    out = nc.dram_tensor("out_0_dram", shape, F32, kind="ExternalOutput").ap()
    build(nc, *args, out)
    r = run_bass_kernel_spmd(nc, [arrays], core_ids=[0])
    return r.results[0]["out_0_dram"]
```
